# Optimizing a Trainium2 kernel written in Bass

```python
import numpy as np
import jax
import jax.numpy as jnp

def _softmax(x, axis=-1):
    return jax.nn.softmax(x, axis=axis)

def _gelu(x):
    return jax.nn.gelu(x, approximate=True)

def _silu(x):
    return jax.nn.silu(x)

def _sigmoid(x):
    return jax.nn.sigmoid(x)

def _layernorm(x, axis=-1, eps=1e-05):
    m = jnp.mean(x, axis=axis, keepdims=True)
    v = jnp.var(x, axis=axis, keepdims=True)
    return (x - m) / jnp.sqrt(v + eps)

def _scatter_add(tgt, idx, src, axis=0):
    return tgt.at[idx].add(src)

def _segment_sum(src, seg, n):
    return jax.ops.segment_sum(src, seg, n)
kernel_name = 'mk_conv_attn_hybrid_d2_conv_nchw256_r4_91917a'

def setup_inputs(seed: int=0):
    np.random.seed(seed)
    _w = jnp.asarray

    def _rec_inputs():
        import jax
        import jax.numpy as jnp
        _gk = jax.random.key(seed)
        x = 7.22e-05 + 1 * jax.random.normal(jax.random.fold_in(_gk, 1), (32, 64, 32, 32), jnp.float32)
        return x
    x = _rec_inputs()

    def _L0_conv_setup():
        import jax, jax.numpy as jnp
        import numpy as np
        B, C, H, W = (32, 64, 32, 32)
        IC, MC, OC = (16, 16, 64)
        key = jax.random.key(seed)
        k = jax.random.split(key, 7)
        s = 1.0 / np.sqrt(C)
        s2 = 1.0 / np.sqrt(IC * MC)
        return {'x': jax.random.normal(k[0], (B, C, H, W), dtype=jnp.float32), 'info_w': jax.random.uniform(k[1], (IC, C), jnp.float32, -s, s), 'info_b': jax.random.uniform(k[2], (IC,), jnp.float32, -s, s), 'mask_w': jax.random.uniform(k[3], (MC, C), jnp.float32, -s, s), 'mask_b': jax.random.uniform(k[4], (MC,), jnp.float32, -s, s), 'out_w': jax.random.uniform(k[5], (OC, IC * MC), jnp.float32, -s2, s2), 'out_b': jax.random.uniform(k[6], (OC,), jnp.float32, -s2, s2)}
    _L0_conv_all = _L0_conv_setup()
    _L0_conv_in = {k: v for k, v in _L0_conv_all.items() if k in ('info_w', 'info_b', 'mask_w', 'mask_b', 'out_w', 'out_b')}
    del _L0_conv_all

    def _L1_attn_setup():
        import jax, jax.numpy as jnp
        import numpy as np
        NHEAD = 8
        ATT_EPS = 1e-06
        LN_EPS = 1e-05

        def _layernorm(x, g, b):
            mu = jnp.mean(x, axis=-1, keepdims=True)
            var = jnp.mean(jnp.square(x - mu), axis=-1, keepdims=True)
            return (x - mu) * jax.lax.rsqrt(var + LN_EPS) * g + b
        key = jax.random.key(seed)
        ks = jax.random.split(key, 7)
        N, L, C = (4, 4096, 64)
        s = 1.0 / np.sqrt(C)
        return {'x': jax.random.normal(ks[0], (N, L, C), jnp.float32), 'Wq': jax.random.normal(ks[1], (C, C), jnp.float32) * s, 'Wk': jax.random.normal(ks[2], (C, C), jnp.float32) * s, 'Wv': jax.random.normal(ks[3], (C, C), jnp.float32) * s, 'Wm': jax.random.normal(ks[4], (C, C), jnp.float32) * s, 'W1': jax.random.normal(ks[5], (2 * C, 2 * C), jnp.float32) * (1.0 / np.sqrt(2 * C)), 'W2': jax.random.normal(ks[6], (2 * C, C), jnp.float32) * (1.0 / np.sqrt(2 * C)), 'g1': jnp.ones((C,), jnp.float32), 'b1': jnp.zeros((C,), jnp.float32), 'g2': jnp.ones((C,), jnp.float32), 'b2': jnp.zeros((C,), jnp.float32)}
    _L1_attn_all = _L1_attn_setup()
    _L1_attn_in = {k: v for k, v in _L1_attn_all.items() if k in ('Wq', 'Wk', 'Wv', 'Wm', 'W1', 'W2', 'g1', 'b1', 'g2', 'b2')}
    del _L1_attn_all

    def _L1_ffn_setup():
        import jax, jax.numpy as jnp
        import numpy as np
        B, T, D, H, E = (16, 1024, 64, 128, 8)
        key = jax.random.key(seed)
        ks = jax.random.split(key, 5)
        x = jax.random.normal(ks[0], (B, T, D), dtype=jnp.float32)
        gate_w = jax.random.normal(ks[1], (D, E), dtype=jnp.float32) * 0.02
        gate_b = jnp.zeros((E,), dtype=jnp.float32)
        W1 = jax.random.normal(ks[2], (E, D, H), dtype=jnp.float32) * 0.02
        b1 = jnp.zeros((E, H), dtype=jnp.float32)
        W2 = jax.random.normal(ks[3], (E, H, D), dtype=jnp.float32) * 0.02
        b2 = jnp.zeros((E, D), dtype=jnp.float32)
        return {'x': x, 'gate_w': gate_w, 'gate_b': gate_b, 'W1': W1, 'b1': b1, 'W2': W2, 'b2': b2}
    _L1_ffn_all = _L1_ffn_setup()
    _L1_ffn_in = {k: v for k, v in _L1_ffn_all.items() if k in ('gate_w', 'gate_b', 'W1', 'b1', 'W2', 'b2')}
    del _L1_ffn_all
    return {'x': x, 'L0_conv_info_w': _L0_conv_in['info_w'], 'L0_conv_info_b': _L0_conv_in['info_b'], 'L0_conv_mask_w': _L0_conv_in['mask_w'], 'L0_conv_mask_b': _L0_conv_in['mask_b'], 'L0_conv_out_w': _L0_conv_in['out_w'], 'L0_conv_out_b': _L0_conv_in['out_b'], 'L1_attn_Wq': _L1_attn_in['Wq'], 'L1_attn_Wk': _L1_attn_in['Wk'], 'L1_attn_Wv': _L1_attn_in['Wv'], 'L1_attn_Wm': _L1_attn_in['Wm'], 'L1_attn_W1': _L1_attn_in['W1'], 'L1_attn_W2': _L1_attn_in['W2'], 'L1_attn_g1': _L1_attn_in['g1'], 'L1_attn_b1': _L1_attn_in['b1'], 'L1_attn_g2': _L1_attn_in['g2'], 'L1_attn_b2': _L1_attn_in['b2'], 'L1_ffn_gate_w': _L1_ffn_in['gate_w'], 'L1_ffn_gate_b': _L1_ffn_in['gate_b'], 'L1_ffn_W1': _L1_ffn_in['W1'], 'L1_ffn_b1': _L1_ffn_in['b1'], 'L1_ffn_W2': _L1_ffn_in['W2'], 'L1_ffn_b2': _L1_ffn_in['b2']}

def reference(x, L0_conv_info_w, L0_conv_info_b, L0_conv_mask_w, L0_conv_mask_b, L0_conv_out_w, L0_conv_out_b, L1_attn_Wq, L1_attn_Wk, L1_attn_Wv, L1_attn_Wm, L1_attn_W1, L1_attn_W2, L1_attn_g1, L1_attn_b1, L1_attn_g2, L1_attn_b2, L1_ffn_gate_w, L1_ffn_gate_b, L1_ffn_W1, L1_ffn_b1, L1_ffn_W2, L1_ffn_b2):
    import jax
    import jax.numpy as jnp

    def _L0_conv_ref(x, info_w, info_b, mask_w, mask_b, out_w, out_b):
        import jax, jax.numpy as jnp
        import numpy as np
        B, C, H, W = (32, 64, 32, 32)
        IC, MC, OC = (16, 16, 64)
        info = jax.nn.relu(jnp.einsum('ic,bchw->bihw', info_w, x) + info_b[None, :, None, None])
        mask = jax.nn.sigmoid(jnp.einsum('mc,bchw->bmhw', mask_w, x) + mask_b[None, :, None, None])
        expanded = (mask[:, :, None, :, :] * info[:, None, :, :, :]).reshape(x.shape[0], MC * IC, x.shape[2], x.shape[3])
        out = jax.nn.relu(jnp.einsum('oe,behw->bohw', out_w, expanded) + out_b[None, :, None, None])
        return out

    def _L1_attn_ref(x, Wq, Wk, Wv, Wm, W1, W2, g1, b1, g2, b2):
        import jax, jax.numpy as jnp
        import numpy as np
        NHEAD = 8
        ATT_EPS = 1e-06
        LN_EPS = 1e-05

        def _layernorm(x, g, b):
            mu = jnp.mean(x, axis=-1, keepdims=True)
            var = jnp.mean(jnp.square(x - mu), axis=-1, keepdims=True)
            return (x - mu) * jax.lax.rsqrt(var + LN_EPS) * g + b
        N, L, C = x.shape
        H = NHEAD
        D = C // H
        q = (x @ Wq).reshape(N, L, H, D)
        k = (x @ Wk).reshape(N, L, H, D)
        v = (x @ Wv).reshape(N, L, H, D)
        Q = jax.nn.elu(q) + 1.0
        K = jax.nn.elu(k) + 1.0
        v = v / L
        KV = jnp.einsum('nshd,nshv->nhdv', K, v)
        Z = 1.0 / (jnp.einsum('nlhd,nhd->nlh', Q, K.sum(axis=1)) + ATT_EPS)
        msg = jnp.einsum('nlhd,nhdv,nlh->nlhv', Q, KV, Z) * L
        msg = msg.reshape(N, L, C) @ Wm
        msg = _layernorm(msg, g1, b1)
        h = jnp.concatenate([x, msg], axis=-1) @ W1
        h = jax.nn.relu(h) @ W2
        msg = _layernorm(h, g2, b2)
        return x + msg

    def _L1_ffn_ref(x, gate_w, gate_b, W1, b1, W2, b2):
        import jax, jax.numpy as jnp
        import numpy as np
        B, T, D, H, E = (16, 1024, 64, 128, 8)
        Bb, Tt, Dd = x.shape
        Ee = gate_w.shape[1]
        xf = x.reshape(-1, Dd)
        N = xf.shape[0]
        logits = xf @ gate_w + gate_b
        probs = jax.nn.softmax(logits, axis=-1)
        top2_vals, top2_idx = jax.lax.top_k(probs, 2)
        cw = jnp.zeros((N, Ee), dtype=xf.dtype).at[jnp.arange(N)[:, None], top2_idx].add(top2_vals)

        def step(acc, params):
            w1, bb1, w2, bb2, we = params
            h = jax.nn.gelu(xf @ w1 + bb1, approximate=False)
            y = h @ w2 + bb2
            return (acc + we[:, None] * y, None)
        out, _ = jax.lax.scan(step, jnp.zeros_like(xf), (W1, b1, W2, b2, cw.T))
        return out.reshape(Bb, Tt, Dd)

    def _gn(v, G=32, eps=1e-05):
        B_, C_, H_, W_ = v.shape
        g = v.reshape(B_, G, C_ // G, H_, W_)
        m = jnp.mean(g, axis=(2, 3, 4), keepdims=True)
        s = jnp.var(g, axis=(2, 3, 4), keepdims=True)
        return ((g - m) / jnp.sqrt(s + eps)).reshape(v.shape)

    def _ln_c(v, eps=1e-06):
        m = jnp.mean(v, axis=1, keepdims=True)
        s = jnp.var(v, axis=1, keepdims=True)
        return (v - m) / jnp.sqrt(s + eps)

    def _ln_t(v, eps=1e-05):
        m = jnp.mean(v, axis=-1, keepdims=True)
        s = jnp.var(v, axis=-1, keepdims=True)
        return (v - m) / jnp.sqrt(s + eps)

    def _to_tokens(v):
        B_, C_, H_, W_ = v.shape
        return v.reshape(B_, C_, H_ * W_).transpose(0, 2, 1)

    def _from_tokens(t, like):
        B_, C_, H_, W_ = like.shape
        return t.transpose(0, 2, 1).reshape(B_, C_, H_, W_)
    x = x + _L0_conv_ref(_gn(x), L0_conv_info_w, L0_conv_info_b, L0_conv_mask_w, L0_conv_mask_b, L0_conv_out_w, L0_conv_out_b)
    t = _to_tokens(x)
    t = t + _L1_attn_ref(_ln_t(t), L1_attn_Wq, L1_attn_Wk, L1_attn_Wv, L1_attn_Wm, L1_attn_W1, L1_attn_W2, L1_attn_g1, L1_attn_b1, L1_attn_g2, L1_attn_b2)
    t = t + _L1_ffn_ref(_ln_t(t), L1_ffn_gate_w, L1_ffn_gate_b, L1_ffn_W1, L1_ffn_b1, L1_ffn_W2, L1_ffn_b2)
    x = _from_tokens(t, x)
    return x

_drawn_inputs = setup_inputs


def setup_inputs(seed=0):
    import zlib

    import numpy as np

    out = dict(_drawn_inputs(seed))
    spreads = {'L1_attn_g1': (1.0, 0.2),
     'L1_attn_b1': (0.0, 0.1),
     'L1_attn_g2': (1.0, 0.2),
     'L1_attn_b2': (0.0, 0.1),
     'L1_ffn_gate_b': (0.0, 0.8),
     'L1_ffn_b1': (0.0, 0.8),
     'L1_ffn_b2': (0.0, 0.8)}
    factors = {'L0_conv_mask_w': 2.686, 'L1_ffn_gate_w': 6.185, 'L1_ffn_W1': 8.0, 'L1_ffn_W2': 8.0}
    for name, (base, spread) in spreads.items():
        noise = np.random.default_rng([zlib.crc32(name.encode()), seed]).standard_normal(out[name].shape)
        drawn = base * np.exp(spread * noise) if base else spread * noise
        out[name] = jnp.asarray(drawn.astype(out[name].dtype))
    for name, factor in factors.items():
        out[name] = (out[name] * factor).astype(out[name].dtype)
    return out
```

```python
from contextlib import ExitStack

import numpy as np

import concourse.bass as bass
from concourse import mybir

F32 = mybir.dt.float32
F32R = mybir.dt.float32r
ALU = mybir.AluOpType
ACT = mybir.ActivationFunctionType
AX_X = mybir.AxisListType.X

P = 128
C = 64
IMGS = 32
T = 1024
PAIRS = IMGS // 2
G = 4
ITERS = PAIRS // G
CH = 512
NCH = T // CH
TB = T // P
IC = 16
E = 8
HD = 8
HID = 128
EP = E // 2
STEPS = 2 * EP
VW = P + 2
LN_EPS = 1e-5
ATT_EPS = 1e-6
LNS = 4

COLS = {}
_at = 0
for _name, _width in [
    ("wim", 64), ("ow", 2 * C), ("center", P), ("mean", P), ("wq", P), ("wk", P), ("wv", P),
    ("wm_t", P), ("w1", HID), ("w2_t", HID), ("headmask", P), ("pairavg", P), ("ident", P),
    ("fold", C), ("w2e", E * C), ("gw", E), ("gb", 2 * TB * E), ("rank", 2 * TB * E), ("cols", 32),
]:
    COLS[_name] = (_at, _width)
    _at += _width
NW = _at
B_IM, B_OUT, G1, B1, G2, B2, EPS, AEPS, B1E, B2E = 0, 1, 2, 3, 4, 5, 6, 7, 8, 16
NREP = 6
NSEL = 2 * EP
ROUTER = 16


def build(nc, x, wpack, w1e, reps, out):
    xd = x.rearrange("(n two) c t -> n (two c) t", two=2)
    od = out.rearrange("(n two) c t -> n (two c) t", two=2)
    with ExitStack() as ctx:
        def sb(name, shape, dt=F32):
            return ctx.enter_context(nc.sbuf_tensor(name, shape, dt))

        def sem(name):
            return ctx.enter_context(nc.semaphore(name))

        def sems(name):
            return [sem(f"{name}{g}") for g in range(G)]

        W = sb("W", [P, NW])
        X = sb("X", [P, G, T])
        XN = sb("XN", [P, G, T])
        T1 = sb("T1", [P, G, T])
        T2 = sb("T2", [P, G, T])
        BIG = sb("BIG", [P, G, 4, T])
        S = sb("S", [P, G, 2, T], F32R)
        CT = sb("CT", [P, 2, T], F32R)
        CHL = sb("CHL", [P, G, 2, P])
        KVM = sb("KVM", [P, G, 2, P])
        WMC = sb("WMC", [P, P])
        W2C = sb("W2C", [P, C])
        W1G = sb("W1G", [P, HID])
        BH = sb("BH", [P, 1])
        BT = sb("BT", [P, 1])
        WEH = sb("WEH", [P, E, HID], F32R)
        WEL = sb("WEL", [P, E, HID], F32R)
        GWH = sb("GWH", [P, E], F32R)
        GWL = sb("GWL", [P, E], F32R)
        REP = sb("REP", [P, NREP + NSEL, P], F32R)
        ST = sb("ST", [P, G, 32])
        R = [ctx.enter_context(nc.psum_tensor(f"R{g}", [P, T], F32)) for g in range(G)]

        def w(name, rows=slice(0, P)):
            a, n = COLS[name]
            return W[rows, a:a + n]

        def col(k, rows=slice(0, P)):
            a = COLS["cols"][0] + k
            return W[rows, a:a + 1]

        def half(c):
            return slice(c * CH, (c + 1) * CH)

        def img(k):
            return slice(k * C, (k + 1) * C)

        Q = [BIG[:, g, 0, :] for g in range(G)]
        K = [BIG[:, g, 1, :] for g in range(G)]
        V = [BIG[:, g, 2:4, :].rearrange("p a t -> p (a t)")[:, 0:TB * VW].rearrange("p (j c) -> p j c", c=VW)
             for g in range(G)]
        U = [[BIG[:, g, k, :] for k in range(2)] for g in range(G)]
        HA = [[BIG[:, g, 2 + k, :] for k in range(2)] for g in range(G)]
        H = [BIG[:, 0, k, :] for k in range(4)]
        ACC = [BIG[:, 1, k, :] for k in range(4)]
        TM = [BIG[:, 2, k, :] for k in range(2)]
        CW = [BIG[:, 3, k, :] for k in range(2)]

        w_in = sem("w_in")
        ct_zero = sem("ct_zero")
        prep_split = sem("prep_split")
        prep_pe = sem("prep_pe")
        prep_done = sem("prep_done")
        x_in = sems("x_in")
        gn_part = sem("gn_part")
        gn_stat = sem("gn_stat")
        gn_dev = sem("gn_dev")
        gn_avg = sem("gn_avg")
        gn_var = sem("gn_var")
        gn_rstd = sem("gn_rstd")
        gn_ln = sem("gn_ln")
        gn_done = sem("gn_done")
        im_ps = sem("im_ps")
        im_act = sem("im_act")
        hl_high = sem("hl_high")
        hl_done = sem("hl_done")
        rep_ps = sem("rep_ps")
        ir_done = sem("ir_done")
        prod_done = sem("prod_done")
        oc_ps = sem("oc_ps")
        oc_act = sem("oc_act")
        x1_done = sem("x1_done")
        ln_ps = sem("ln_ps")
        ln_sq = sem("ln_sq")
        ln_cp = sem("ln_cp")
        ln_var = sem("ln_var")
        ln_log = sem("ln_log")
        ln_rstd = sem("ln_rstd")
        ln_done = sem("ln_done")
        qk_ps = sem("qk_ps")
        qk_exp = sem("qk_exp")
        qk_min = sem("qk_min")
        qk_done = sem("qk_done")
        v_ps = sem("v_ps")
        v_done = sem("v_done")
        kv_ps = sem("kv_ps")
        kv_done = sem("kv_done")
        den_ps = sem("den_ps")
        den_log = sem("den_log")
        den_done = sem("den_done")
        num_ps = sem("num_ps")
        msg_done = sem("msg_done")
        u_in = sems("u_in")
        h_ps = sem("h_ps")
        h_done = sem("h_done")
        y2_done = sem("y2_done")
        x2_done = sem("x2_done")
        ln_mul = sem("ln_mul")
        sp_high = sem("sp_high")
        s_in = sems("s_in")
        gate_ps = sem("gate_ps")
        lg_done = sem("lg_done")
        lg_shifted = sem("lg_shifted")
        gate_exp = sem("gate_exp")
        cw_done = sem("cw_done")
        cwt_ps = sem("cwt_ps")
        cwt_done = sem("cwt_done")
        ct_in = [sem(f"ct_in{b}") for b in range(2)]
        l1_ps = sem("l1_ps")
        gelu_done = sem("gelu_done")
        cwb_ps = sem("cwb_ps")
        cwb_done = sem("cwb_done")
        y_ps = sem("y_ps")
        comb_done = sem("comb_done")
        acc_done = sem("acc_done")
        fin_ps = sem("fin_ps")
        fin_done = sem("fin_done")
        out_done = sems("out_done")
        ones_set = sem("ones_set")
        dve_prep = sem("dve_prep")
        router = sem("router")
        ct_high = sem("ct_high")

        def nth(n, g):
            return (n - 1) * G + g + 1

        US = G * STEPS
        ADDS = STEPS - 2

        def adds(u):
            return u // EP * (EP - 1) + max(u % EP - 1, 0)

        def gt(k):
            return T1[:, :, P * k:P * k + P]

        def rows(t):
            return t.rearrange("p g (r e) -> p g r e", e=E)

        block = ctx.enter_context(nc.Block())

        @block.sync
        def _(sp):
            sp.dma_start(W[:, :], wpack).then_inc(w_in, 16)
            sp.dma_start(BIG[:, 0, 0, :], w1e).then_inc(w_in, 16)
            sp.dma_start(BIG[:, 0, 1:3, :].rearrange("p a t -> p (a t)")[:, 0:(NREP + NSEL) * P],
                         reps).then_inc(w_in, 16)
            for g in range(G):
                sp.dma_start(X[:, g, :], xd[g]).then_inc(x_in[g], 16)

            def iteration(i, load_next):
                for g in range(G):
                    sp.wait_ge(ln_done, nth(i * LNS + 2, g))
                    for k in range(2):
                        sp.dma_start(U[g][k][0:C, :], XN[img(k), g, :]).then_inc(u_in[g], 16)
                        sp.dma_start(U[g][k][C:P, :], T2[img(k), g, :]).then_inc(u_in[g], 16)
                for g in range(G):
                    sp.wait_ge(ln_done, nth(i * LNS + 4, g))
                    for k in range(2):
                        sp.dma_start(S[0:C, g, k, :].bitcast(F32), XN[img(k), g, :]).then_inc(s_in[g], 16)
                        sp.dma_start(S[C:P, g, k, :].bitcast(F32), T2[img(k), g, :]).then_inc(s_in[g], 16)
                sp.wait_ge(cwt_done, i + 1)
                for g in range(G):
                    if g >= 2:
                        sp.wait_ge(cwb_ps, i * US + (g - 1) * STEPS)
                    for part in range(2):
                        sp.dma_start(
                            CT[16 * part:16 * part + 16, g % 2, :].bitcast(F32),
                            CHL[:, g, part, :]).then_inc(ct_in[g % 2], 16)
                    if g >= 1:
                        store(i, g - 1, load_next)
                store(i, G - 1, load_next)

            def store(i, g, load_next):
                sp.wait_ge(fin_done, i * G + g + 1)
                sp.dma_start(od[i * G + g], X[:, g, :]).then_inc(out_done[g], 16)
                if load_next:
                    sp.wait_ge(out_done[g], i * 16 + 16)
                    sp.dma_start(X[:, g, :], xd[i * G + G + g]).then_inc(x_in[g], 16)

            with sp.Fori(0, ITERS - 1) as i:
                iteration(i, True)
            iteration(ITERS - 1, False)
            for g in range(G):
                sp.wait_ge(out_done[g], ITERS * 16)

        @block.tensor
        def _(pe):
            mm = nc.tensor.matmul

            def cover(dst, lhsT, rhs):
                for c in range(NCH):
                    last = mm(dst[:, half(c)], lhsT, rhs[:, half(c)], start=True, stop=True)
                return last

            pe.wait_ge(w_in, 48)
            mm(R[0][:, 0:P], w("wm_t"), w("center"), start=True, stop=True).then_inc(prep_pe, 1)
            mm(R[1][:, 0:C], w("w2_t"), w("center")[:, 0:C], start=True, stop=True).then_inc(prep_pe, 1)
            mm(R[2][:, 0:1], w("w1"), col(B1), start=True, stop=True).then_inc(prep_pe, 1)
            pe.wait_ge(prep_done, 1)

            with pe.Fori(0, ITERS) as i:
                def norm(g, k):
                    pe.wait_ge(ln_sq, nth(i * LNS + k, g))
                    cover(R[g], w("mean"), T1[:, g, :]).then_inc(ln_var, 1)

                for g in range(G):
                    pe.wait_ge(gn_stat, nth(i + 1, g))
                    mm(R[g][:, 0:2], w("pairavg"), ST[:, g, 12:14], start=True, stop=True).then_inc(gn_avg, 1)
                for g in range(G):
                    pe.wait_ge(gn_done, nth(i + 1, g))
                    cover(R[g][0:C, :], w("wim"), XN[:, g, :]).then_inc(im_ps, 1)
                for u in range(NREP):
                    for g in range(G):
                        if u == 0:
                            pe.wait_ge(hl_done, nth(i + 1, g))
                        elif u % 3 == 1:
                            pe.wait_ge(ir_done, nth(i * 2 + u // 3 + 1, g))
                        else:
                            pe.wait_ge(prod_done, nth(i * 4 + (u + 1) // 3 + u // 3, g))
                        cover(R[g], REP[:, u, :], S[:, g, 0, :]).then_inc(rep_ps, 1)
                for g in range(G):
                    pe.wait_ge(prod_done, nth(i * 4 + 4, g))
                    for c in range(NCH):
                        for h in range(2):
                            for k in range(2):
                                last = mm(R[g][img(k), half(c)], w("ow")[:, C * h:C * h + C],
                                          BIG[:, g, 2 * k + h, half(c)], start=(h == 0), stop=(h == 1))
                    last.then_inc(oc_ps, 1)
                for g in range(G):
                    pe.wait_ge(x1_done, nth(i + 1, g))
                    cover(R[g], w("center"), X[:, g, :]).then_inc(ln_ps, 1)
                for g in range(G):
                    norm(g, 1)
                for g in range(G):
                    pe.wait_ge(ln_done, nth(i * LNS + 1, g))
                    cover(R[g], w("wq"), XN[:, g, :]).then_inc(qk_ps, 1)
                for g in range(G):
                    pe.wait_ge(qk_done, nth(i * 2 + 1, g))
                    for j in range(TB):
                        last = mm(R[g][:, P * j:P * j + P], XN[:, g, P * j:P * j + P], w("wk"),
                                  start=True, stop=True)
                    last.then_inc(qk_ps, 1)
                for g in range(G):
                    pe.wait_ge(qk_done, nth(i * 2 + 2, g))
                    for j in range(TB):
                        last = mm(R[g][:, P * j:P * j + P], XN[:, g, P * j:P * j + P], w("wv"),
                                  start=True, stop=True)
                    last.then_inc(v_ps, 1)
                for g in range(G):
                    pe.wait_ge(v_done, nth(i + 1, g))
                    pe.wait_ge(ones_set, nth(i + 1, g))
                    for j in range(TB):
                        last = mm(R[g][:, 0:VW], K[g][:, P * j:P * j + P], V[g][:, j, :],
                                  start=(j == 0), stop=(j == TB - 1))
                    last.then_inc(kv_ps, 1)
                for g in range(G):
                    pe.wait_ge(kv_done, nth(i + 1, g))
                    cover(R[g], KVM[:, g, 1, :], Q[g]).then_inc(den_ps, 1)
                for g in range(G):
                    pe.wait_ge(den_done, nth(i + 1, g))
                    cover(R[g], KVM[:, g, 0, :], Q[g]).then_inc(num_ps, 1)
                for g in range(G):
                    pe.wait_ge(msg_done, nth(i + 1, g))
                    cover(R[g], WMC[:, :], T2[:, g, :]).then_inc(ln_ps, 1)
                for g in range(G):
                    norm(g, 2)
                for k in range(2):
                    for g in range(G):
                        if k == 0:
                            pe.wait_ge(u_in[g], i * 64 + 64)
                        else:
                            pe.wait_ge(h_done, nth(i * 2 + 1, g))
                        cover(R[g], W1G[:, :], U[g][k]).then_inc(h_ps, 1)
                for g in range(G):
                    pe.wait_ge(h_done, nth(i * 2 + 2, g))
                    for c in range(NCH):
                        for k in range(2):
                            last = mm(R[g][img(k), half(c)], W2C[:, :], HA[g][k][:, half(c)],
                                      start=True, stop=True)
                    last.then_inc(ln_ps, 1)
                for g in range(G):
                    norm(g, 3)
                for g in range(G):
                    pe.wait_ge(x2_done, nth(i + 1, g))
                    cover(R[g], w("center"), X[:, g, :]).then_inc(ln_ps, 1)
                for g in range(G):
                    norm(g, 4)
                for g in range(G):
                    pe.wait_ge(s_in[g], i * 64 + 64)
                    for k in range(2):
                        for j in range(TB):
                            o = (k * TB + j) * E
                            for n, gw in enumerate((GWH, GWL)):
                                last = mm(R[g][:, o:o + E], S[:, g, k, P * j:P * j + P], gw[:, :],
                                          start=(n == 0), stop=(n == 1))
                    last.then_inc(gate_ps, 1)

                def second(u):
                    if u >= 1:
                        pe.wait_ge(comb_done, i * US + u)
                    if u >= 1 and u % STEPS == 0:
                        pe.wait_ge(fin_done, i * G + u // STEPS)
                    pe.wait_ge(gelu_done, i * 2 * US + 2 * u + 2)
                    for c in range(NCH):
                        for e in range(2):
                            ex = 2 * (u % EP) + e
                            last = mm(R[2][img(e), half(c)], w("w2e")[:, C * ex:C * ex + C],
                                      H[2 * (u % 2) + e][:, half(c)], start=True, stop=True)
                    last.then_inc(y_ps, 1)

                def finish(g):
                    pe.wait_ge(comb_done, i * US + (g + 1) * STEPS)
                    pe.wait_ge(acc_done, i * G * ADDS + (g + 1) * ADDS)
                    for c in range(NCH):
                        for k in range(2):
                            last = mm(R[2][img(k), half(c)], w("fold"), ACC[2 * (g % 2) + k][:, half(c)],
                                      start=True, stop=True)
                    last.then_inc(fin_ps, 1)

                for u in range(US):
                    g, k, ep = u // STEPS, u // EP % 2, u % EP
                    for e in range(2):
                        if u >= 1:
                            pe.wait_ge(gelu_done, i * 2 * US + 2 * (u - 1) + e + 1)
                        else:
                            pe.wait_ge(lg_done, nth(i + 1, e))
                        ex = 2 * ep + e
                        for c in range(NCH):
                            mm(R[e][:, half(c)], WEH[:, ex, :], S[:, g, k, half(c)], start=True, stop=False)
                            last = mm(R[e][:, half(c)], WEL[:, ex, :], S[:, g, k, half(c)],
                                      start=False, stop=True)
                        last.then_inc(l1_ps, 1)
                    if u == 0:
                        pe.wait_ge(lg_done, nth(i + 1, G - 1))
                        pe.wait_ge(cw_done, i + 1)
                        for s in range(G):
                            last = nc.tensor.transpose(R[3][:, P * s:P * s + P], T1[:, s, 0:P], w("ident"))
                        last.then_inc(cwt_ps, 1)
                        pe.wait_ge(cwt_done, i + 1)
                    if u >= STEPS + 1 and u % STEPS == 1:
                        finish(u // STEPS - 1)
                    if u % STEPS == 0:
                        pe.wait_ge(ct_in[g % 2], (i * (G // 2) + g // 2 + 1) * 32)
                    if u >= 1:
                        pe.wait_ge(cwb_done, i * US + u)
                    cover(R[3], REP[:, NREP + k * EP + ep, :], CT[:, g % 2, :]).then_inc(cwb_ps, 1)
                    if u >= 1:
                        second(u - 1)
                second(US - 1)
                finish(G - 1)

        @block.scalar
        def _(act):
            a = nc.scalar.activation
            act.wait_ge(w_in, 48)
            a(BT[:, :], col(B_IM), ACT.Copy, scale=0.5).then_inc(prep_split, 1)
            act.wait_ge(prep_done, 1)
            act.wait_ge(prep_split, 1)

            with act.Fori(0, ITERS) as i:
                def rstd(g, k, src, dst, log, done, per):
                    a(dst, src, ACT.Ln, bias=col(EPS)).then_inc(log, 1)
                    act.wait_ge(log, nth(i * per + k, g))
                    a(dst, dst, ACT.Exp, scale=-0.5).then_inc(done, 1)

                def norm(k):
                    for g in range(G):
                        act.wait_ge(ln_cp, nth(i * LNS + k, g))
                        a(T1[:, g, :], T2[:, g, :], ACT.Square).then_inc(ln_sq, 1)
                    for g in range(G):
                        act.wait_ge(ln_var, nth(i * LNS + k, g))
                        rstd(g, k, R[g][:, :], T1[:, g, :], ln_log, ln_rstd, LNS)

                nc.scalar.preload_act_table_set("natural_log_exp_and_others")
                for g in range(G):
                    act.wait_ge(gn_var, nth(i + 1, g))
                    rstd(g, 1, ST[:, g, 20:21], ST[:, g, 21:22], gn_ln, gn_rstd, 1)
                nc.scalar.preload_act_table_set("exp_and_others")
                for g in range(G):
                    act.wait_ge(im_ps, nth(i + 1, g))
                    a(T1[0:32, g, :], R[g][0:32, :], ACT.Relu, bias=col(B_IM, slice(0, 32)))
                    a(T1[32:64, g, :], R[g][32:64, :], ACT.Tanh, bias=BT[32:64, :], scale=0.5)\
                        .then_inc(im_act, 1)
                for k in range(2):
                    for g in range(G):
                        act.wait_ge(rep_ps, nth(i * NREP + 3 * k + 1, g))
                        a(T2[:, g, :], R[g][:, :], ACT.Copy).then_inc(ir_done, 1)
                for g in range(G):
                    act.wait_ge(oc_ps, nth(i + 1, g))
                    a(T1[:, g, :], R[g][:, :], ACT.Relu, bias=col(B_OUT), scale=0.5).then_inc(oc_act, 1)
                nc.scalar.preload_act_table_set("natural_log_exp_and_others")
                norm(1)
                for k in range(2):
                    for g in range(G):
                        act.wait_ge(qk_ps, nth(i * 2 + k + 1, g))
                        a(T1[:, g, :], R[g][:, :], ACT.Exp).then_inc(qk_exp, 1)
                for g in range(G):
                    act.wait_ge(v_ps, nth(i + 1, g))
                    a(V[g][:, :, 0:P], R[g][:, :].rearrange("p (j c) -> p j c", c=P), ACT.Copy)\
                        .then_inc(v_done, 1)
                for g in range(G):
                    act.wait_ge(den_ps, nth(i + 1, g))
                    a(T1[:, g, :], R[g][:, :], ACT.Ln, bias=col(AEPS)).then_inc(den_log, 1)
                for g in range(G):
                    act.wait_ge(den_log, nth(i + 1, g))
                    a(T1[:, g, :], T1[:, g, :], ACT.Exp, scale=-1.0).then_inc(den_done, 1)
                norm(2)
                for k in range(2):
                    for g in range(G):
                        act.wait_ge(h_ps, nth(i * 2 + k + 1, g))
                        a(HA[g][k], R[g][:, :], ACT.Relu, bias=BH[:, :]).then_inc(h_done, 1)
                norm(3)
                norm(4)
                act.wait_ge(lg_shifted, i + 1)
                a(gt(1), gt(0), ACT.Exp).then_inc(gate_exp, 1)
                nc.scalar.preload_act_table_set("gelu_and_others")
                for u in range(US):
                    for e in range(2):
                        ex = 2 * (u % EP) + e
                        act.wait_ge(l1_ps, i * 2 * US + 2 * u + e + 1)
                        if u >= 2:
                            act.wait_ge(y_ps, i * US + u - 1)
                        a(H[2 * (u % 2) + e], R[e][:, :], ACT.Gelu, bias=col(B1E + ex)).then_inc(gelu_done, 1)
                    act.wait_ge(cwb_ps, i * US + u + 1)
                    if u >= 2:
                        act.wait_ge(comb_done, i * US + u - 1)
                    a(CW[u % 2], R[3][:, :], ACT.Copy).then_inc(cwb_done, 1)

        @block.gpsimd
        def _(pool):
            add = lambda dst, src: nc.gpsimd.tensor_tensor(dst, src, dst, ALU.add)
            nc.gpsimd.memset(CT[:, :, :].bitcast(F32), 0.0).then_inc(ct_zero, 1)

            with pool.Fori(0, ITERS) as i:
                for g in range(G):
                    pool.wait_ge(oc_act, nth(i + 1, g))
                    add(X[:, g, :], T1[:, g, :]).then_inc(x1_done, 1)
                    nc.gpsimd.memset(V[g][:, :, P:VW], 1.0).then_inc(ones_set, 1)
                for g in range(G):
                    pool.wait_ge(y2_done, nth(i + 1, g))
                    add(X[:, g, :], T2[:, g, :]).then_inc(x2_done, 1)
                for u in range(US):
                    if u % EP:
                        pool.wait_ge(comb_done, i * US + u + 1)
                        if u % EP > 1:
                            pool.wait_ge(acc_done, i * G * ADDS + adds(u))
                        add(ACC[2 * (u // STEPS % 2) + u // EP % 2], TM[u % 2]).then_inc(acc_done, 1)

        @block.vector
        def _(dve):
            v = nc.vector

            dve.wait_ge(w_in, 48)
            raw = BIG[:, 0, 0, :].rearrange("p (e h) -> p e h", h=HID)
            v.tensor_copy(WEH[:, :, :], raw).then_inc(dve_prep, 1)
            v.tensor_copy(GWH[:, :], w("gw")).then_inc(dve_prep, 1)
            v.tensor_copy(REP[:, :, :], BIG[:, 0, 1:3, :].rearrange("p a t -> p (a t)")
                          [:, 0:(NREP + NSEL) * P].rearrange("p (n c) -> p n c", c=P)).then_inc(dve_prep, 1)
            dve.wait_ge(dve_prep, 2)
            v.tensor_tensor(WEL[:, :, :], raw, WEH[:, :, :].bitcast(F32), ALU.subtract).then_inc(dve_prep, 1)
            v.tensor_tensor(GWL[:, :], w("gw"), GWH[:, :].bitcast(F32), ALU.subtract).then_inc(dve_prep, 1)
            v.tensor_scalar(W1G[:, :], w("w1"), col(G1), None, ALU.mult).then_inc(dve_prep, 1)
            dve.wait_ge(prep_pe, 3)
            v.tensor_copy(WMC[:, :], R[0][:, 0:P]).then_inc(dve_prep, 1)
            v.tensor_copy(W2C[:, :], R[1][:, 0:C]).then_inc(dve_prep, 1)
            v.tensor_copy(BH[:, :], R[2][:, 0:1]).then_inc(dve_prep, 1)
            dve.wait_ge(dve_prep, 9)
            dve.wait_ge(ct_zero, 1)
            v.memset(ST[:, 0, 30:31], 0.0).then_inc(prep_done, 1)

            with dve.Fori(0, ITERS) as i:
                def norm(k, dst):
                    for g in range(G):
                        dve.wait_ge(ln_ps, nth(i * LNS + k, g))
                        v.tensor_copy(T2[:, g, :], R[g][:, :]).then_inc(ln_cp, 1)
                    if dst is not None:
                        for g in range(G):
                            dve.wait_ge(ln_cp, nth(i * LNS + k, g))
                            dve.wait_ge(ln_rstd, nth(i * LNS + k, g))
                            v.tensor_tensor(dst[:, g, :], T2[:, g, :], T1[:, g, :], ALU.mult)\
                                .then_inc(ln_mul if k == 4 else ln_done, 1)

                for g in range(G):
                    dve.wait_ge(x_in[g], i * 16 + 16)
                    for c in range(NCH):
                        ins = v.bn_stats(ST[:, g, 6 * c:6 * c + 6], X[:, g, half(c)])
                    ins.then_inc(gn_part, 1)
                for g in range(G):
                    dve.wait_ge(gn_part, nth(i + 1, g))
                    v.memset(ST[:, g, 31:32], 0.0)
                    v.bn_aggr(ST[:, g, 12:14], ST[:, g, 0:12]).then_inc(gn_stat, 1)
                for g in range(G):
                    dve.wait_ge(gn_avg, nth(i + 1, g))
                    dve.wait_ge(gn_stat, nth(i + 1, g))
                    v.tensor_tensor(ST[:, g, 14:15], ST[:, g, 12:13], R[g][:, 0:1], ALU.subtract)\
                        .then_inc(gn_dev, 1)
                for g in range(G):
                    dve.wait_ge(gn_dev, nth(i + 1, g))
                    v.scalar_tensor_tensor(out=ST[:, g, 20:21], in0=ST[:, g, 14:15], scalar=ST[:, g, 14:15],
                                           in1=R[g][:, 1:2], op0=ALU.mult, op1=ALU.add).then_inc(gn_var, 1)
                for g in range(G):
                    dve.wait_ge(gn_rstd, nth(i + 1, g))
                    v.tensor_scalar(XN[:, g, :], X[:, g, :], R[g][:, 0:1], ST[:, g, 21:22],
                                    ALU.subtract, ALU.mult).then_inc(gn_done, 1)
                for g in range(G):
                    dve.wait_ge(im_act, nth(i + 1, g))
                    v.tensor_copy(S[0:C, g, 0, :], T1[0:C, g, :]).then_inc(hl_high, 1)
                for g in range(G):
                    dve.wait_ge(hl_high, nth(i + 1, g))
                    v.tensor_tensor(S[C:P, g, 0, :], T1[0:C, g, :], S[0:C, g, 0, :].bitcast(F32),
                                    ALU.subtract).then_inc(hl_done, 1)
                for k in range(2):
                    for h in range(2):
                        for g in range(G):
                            if h == 0:
                                dve.wait_ge(ir_done, nth(i * 2 + k + 1, g))
                            dve.wait_ge(rep_ps, nth(i * NREP + 3 * k + h + 2, g))
                            v.scalar_tensor_tensor(out=BIG[:, g, 2 * k + h, :], in0=R[g][:, :], scalar=1.0,
                                                   in1=T2[:, g, :], op0=ALU.add, op1=ALU.mult)\
                                .then_inc(prod_done, 1)
                norm(1, XN)
                for k, dst in enumerate((Q, K)):
                    for g in range(G):
                        dve.wait_ge(qk_exp, nth(i * 2 + k + 1, g))
                        v.tensor_scalar(T1[:, g, :], T1[:, g, :], 1.0, None, ALU.min).then_inc(qk_min, 1)
                    for g in range(G):
                        dve.wait_ge(qk_min, nth(i * 2 + k + 1, g))
                        v.scalar_tensor_tensor(out=dst[g], in0=R[g][:, :], scalar=0.0, in1=T1[:, g, :],
                                               op0=ALU.max, op1=ALU.add).then_inc(qk_done, 1)
                for g in range(G):
                    dve.wait_ge(kv_ps, nth(i + 1, g))
                    v.tensor_tensor(KVM[:, g, 0, :], R[g][:, 0:P], w("headmask"), ALU.mult)
                    v.tensor_scalar(KVM[:, g, 1, :], w("headmask"), R[g][:, P:P + 1], None, ALU.mult)\
                        .then_inc(kv_done, 1)
                for g in range(G):
                    dve.wait_ge(den_done, nth(i + 1, g))
                    dve.wait_ge(num_ps, nth(i + 1, g))
                    v.tensor_tensor(T2[:, g, :], R[g][:, :], T1[:, g, :], ALU.mult).then_inc(msg_done, 1)
                norm(2, T2)
                norm(3, None)
                for g in range(G):
                    dve.wait_ge(ln_cp, nth(i * LNS + 3, g))
                    dve.wait_ge(ln_rstd, nth(i * LNS + 3, g))
                    v.scalar_tensor_tensor(out=T2[:, g, :], in0=T2[:, g, :], scalar=col(G2), in1=T1[:, g, :],
                                           op0=ALU.mult, op1=ALU.mult).then_inc(ln_done, 1)
                for g in range(G):
                    dve.wait_ge(ln_done, nth(i * LNS + 3, g))
                    v.scalar_tensor_tensor(out=T2[:, g, :], in0=T2[:, g, :], scalar=col(B2), in1=XN[:, g, :],
                                           op0=ALU.add, op1=ALU.add).then_inc(y2_done, 1)
                norm(4, T2)
                for g in range(G):
                    dve.wait_ge(ln_mul, nth(i + 1, g))
                    v.tensor_copy(XN[:, g, :].bitcast(F32R), T2[:, g, :]).then_inc(sp_high, 1)
                for g in range(G):
                    dve.wait_ge(sp_high, nth(i + 1, g))
                    v.tensor_tensor(T2[:, g, :], T2[:, g, :], XN[:, g, :], ALU.subtract).then_inc(ln_done, 1)

                steps = [0]

                def link(ins):
                    steps[0] += 1
                    ins.then_inc(router, 1)
                    dve.wait_ge(router, i * ROUTER + steps[0])

                def per_token(t):
                    return t.unsqueeze(3).broadcast_to([P, G, 2 * TB, E])

                best = T1[:, :, 6 * P:6 * P + 2 * TB]
                for g in range(G):
                    dve.wait_ge(gate_ps, nth(i + 1, g))
                    ins = v.tensor_tensor(T1[:, g, 0:P], R[g][:, 0:P], w("gb"), ALU.add)
                    ins.then_inc(lg_done, 1)
                dve.wait_ge(lg_done, nth(i + 1, G - 1))
                link(v.reduce_max(best, rows(gt(0)), AX_X))
                v.tensor_tensor(rows(gt(0)), rows(gt(0)), per_token(best), ALU.subtract).then_inc(lg_shifted, 1)
                dve.wait_ge(gate_exp, i + 1)

                def pick(values, chosen):
                    link(v.reduce_max(best, rows(values), AX_X))
                    link(v.tensor_tensor(rows(chosen), rows(values), per_token(best), ALU.is_equal))
                    for g in range(G):
                        ins = v.tensor_tensor(chosen[:, g, :], chosen[:, g, :], w("rank"), ALU.mult)
                    link(ins)
                    link(v.reduce_max(best, rows(chosen), AX_X))
                    link(v.tensor_tensor(rows(chosen), rows(chosen), per_token(best), ALU.is_equal))

                pick(gt(1), gt(2))
                link(v.scalar_tensor_tensor(out=gt(3), in0=gt(2), scalar=-2.0, in1=gt(1),
                                            op0=ALU.mult, op1=ALU.add))
                pick(gt(3), gt(4))
                link(v.tensor_tensor(gt(2), gt(2), gt(4), ALU.add))
                link(v.tensor_tensor(gt(2), gt(2), gt(1), ALU.mult))
                link(v.reduce_sum(best, rows(gt(1)), AX_X))
                link(v.reciprocal(best, best))
                for g in range(G):
                    ins = v.tensor_tensor(
                        T1[:, g, 0:P].rearrange("p (k e j) -> p k j e", k=2, e=E),
                        T1[:, g, 2 * P:3 * P].rearrange("p (k j e) -> p k j e", k=2, e=E),
                        best[:, g, :].rearrange("p (k j) -> p k j", k=2).unsqueeze(3)
                        .broadcast_to([P, 2, TB, E]), ALU.mult)
                ins.then_inc(cw_done, 1)
                assert steps[0] == ROUTER
                dve.wait_ge(cwt_ps, i + 1)
                trans = R[3][:, 0:G * P].rearrange("p (g t) -> p g t", g=G)
                v.tensor_copy(CHL[:, :, 0, :].bitcast(F32R), trans).then_inc(ct_high, 1)
                dve.wait_ge(ct_high, i + 1)
                v.tensor_tensor(CHL[:, :, 1, :], trans, CHL[:, :, 0, :], ALU.subtract).then_inc(cwt_done, 1)

                def finish(g):
                    dve.wait_ge(fin_ps, i * G + g + 1)
                    v.tensor_tensor(X[:, g, :], R[2][:, :], X[:, g, :], ALU.add).then_inc(fin_done, 1)

                for u in range(US):
                    ep = u % EP
                    if u >= 1 and u % STEPS == 0:
                        finish(u // STEPS - 1)
                    dve.wait_ge(y_ps, i * US + u + 1)
                    dve.wait_ge(cwb_done, i * US + u + 1)
                    if ep and u >= 2 and (u - 2) % EP:
                        dve.wait_ge(acc_done, i * G * ADDS + adds(u - 1))
                    dst = TM[u % 2] if ep else ACC[2 * (u // STEPS % 2) + u // EP % 2]
                    v.scalar_tensor_tensor(out=dst, in0=R[2][:, :], scalar=col(B2E + ep), in1=CW[u % 2],
                                           op0=ALU.add, op1=ALU.mult).then_inc(comb_done, 1)
                finish(G - 1)


def kernel(**inputs):
    import concourse.bacc as bacc
    from concourse.bass_utils import run_bass_kernel_spmd

    f = lambda n: np.asarray(inputs[n])
    wp = np.zeros((P, NW), np.float32)

    def put(name, a, rows=0, at=0):
        a = np.atleast_2d(a)
        c = COLS[name][0] + at
        wp[rows:rows + a.shape[0], c:c + a.shape[1]] = a

    info, mask, ow = f("L0_conv_info_w"), f("L0_conv_mask_w"), f("L0_conv_out_w")
    wm, w1, w2 = f("L1_attn_Wm"), f("L1_attn_W1"), f("L1_attn_W2")
    centre = np.eye(C, dtype=np.float32) - np.float32(1 / C)
    for k in range(2):
        r = k * C
        put("wim", info.T, r, IC * k)
        put("wim", mask.T, r, 2 * IC + IC * k)
        put("center", centre, r, r)
        put("mean", np.full((C, C), 1 / C, np.float32), r, r)
        put("wq", f("L1_attn_Wq"), r, r)
        put("wk", f("L1_attn_Wk"), r, r)
        put("wv", f("L1_attn_Wv"), r, r)
        put("wm_t", wm.T, r, r)
        put("gw", f("L1_ffn_gate_w"), r)
        put("fold", np.eye(C, dtype=np.float32), r)
        put("cols", f("L0_conv_info_b")[:, None], IC * k, B_IM)
        put("cols", f("L0_conv_mask_b")[:, None], 2 * IC + IC * k, B_IM)
        put("cols", f("L0_conv_out_b")[:, None], r, B_OUT)
        put("cols", f("L1_attn_g2")[:, None], r, G2)
        put("cols", f("L1_attn_b2")[:, None], r, B2)
    for h in range(2):
        put("ow", ow.T[P * h:P * h + P], 0, C * h)
    put("w1", w1)
    put("w2_t", w2.T)
    put("headmask", np.kron(np.eye(P // HD), np.ones((HD, HD))).astype(np.float32))
    put("pairavg", np.kron(np.eye(C), np.full((2, 2), 0.5)).astype(np.float32))
    put("ident", np.eye(P, dtype=np.float32))
    put("cols", np.ones((C, 1), np.float32), 0, G1)
    put("cols", f("L1_attn_g1")[:, None], C, G1)
    put("cols", f("L1_attn_b1")[:, None], C, B1)
    put("cols", np.full((P, 1), LN_EPS, np.float32), 0, EPS)
    put("cols", np.full((P, 1), ATT_EPS, np.float32), 0, AEPS)
    put("gb", np.broadcast_to(np.tile(f("L1_ffn_gate_b"), 2 * TB), (P, 2 * TB * E)))
    put("rank", np.broadcast_to(np.tile(np.arange(E, 0, -1, dtype=np.float32), 2 * TB), (P, 2 * TB * E)))
    we1, we2 = f("L1_ffn_W1"), f("L1_ffn_W2")
    for e in range(E):
        put("w2e", we2[e], 0, C * e)
        put("cols", f("L1_ffn_b1")[e][:, None], 0, B1E + e)
        put("cols", f("L1_ffn_b2")[e][:, None], C * (e % 2), B2E + e // 2)
    w1e = np.concatenate([we1.transpose(1, 0, 2).reshape(C, E * HID)] * 2, axis=0)
    reps = np.zeros((P, NREP + NSEL, P), np.float32)
    for k in range(2):
        for part in range(2):
            for o in range(P):
                reps[C * part + IC * k + o % IC, 3 * k, o] = 1
                for h in range(2):
                    reps[C * part + 2 * IC + IC * k + o // IC + HD * h, 3 * k + 1 + h, o] = 1
                for ep in range(EP):
                    reps[16 * part + E * k + 2 * ep + o // C, NREP + EP * k + ep, o] = 1

    nc = bacc.Bacc("TRN2", target_bir_lowering=False, num_devices=1)
    xs = f("x")
    arrays = {"x": np.ascontiguousarray(xs.reshape(IMGS, C, T)), "wpack": wp,
              "w1e": np.ascontiguousarray(w1e), "reps": reps.reshape(P, -1)}
    aps = [nc.dram_tensor(n, a.shape, F32, kind="ExternalInput").ap() for n, a in arrays.items()]
    out = nc.dram_tensor("out", (IMGS, C, T), F32, kind="ExternalOutput").ap()
    build(nc, *aps, out)
    r = run_bass_kernel_spmd(nc, [arrays], core_ids=[0])
    return r.results[0]["out"].reshape(xs.shape)
```

```python
from contextlib import ExitStack

import numpy as np

import concourse.bass as bass
from concourse import mybir

F32 = mybir.dt.float32
F32R = mybir.dt.float32r
I32 = mybir.dt.int32
ALU = mybir.AluOpType
ACT = mybir.ActivationFunctionType
AX_X = mybir.AxisListType.X

P = 128
C = 64
IMGS = 32
T = 1024
PAIRS = IMGS // 2
G = 2
GROUPS = PAIRS // G
CH = 512
NCH = T // CH
TB = T // P
IC = 16
E = 8
HD = 8
HID = 128
EP = E // 2
CH_UNITS = 2 * EP * 2
US = G * CH_UNITS
VW = P + 2
LN_EPS = 1e-5
ATT_EPS = 1e-6
LNS = 4

COLS = {}
_at = 0
for _name, _width in [
    ("wim", 64), ("ow", 2 * C), ("center", P), ("mean", P), ("wq", P), ("wk", P), ("wv", P),
    ("wm_t", P), ("w1", HID), ("w2_t", HID), ("headmask", P), ("pairavg", P), ("ident", P),
    ("fold", C), ("w2e", E * C), ("gw", 2 * E), ("gb", 2 * TB * E), ("rank", 2 * TB * E), ("cols", 32),
]:
    COLS[_name] = (_at, _width)
    _at += _width
NW = _at
B_IM, B_OUT, G1, B1, G2, B2, B1E, B2E = 0, 1, 2, 3, 4, 5, 8, 16
NREP = 6
NSEL = 2 * EP
NORMS = 2 * TB
FAR = 1e30
HEADS = P // HD
RSQRT_GUESS = float(0x5F3759DF - 0x400000 - 0x80000000)

SCHEDULE = [
    ("channel_stats", 1), ("group_stats", 1), ("group_norm", 0), ("info_mask", 1), ("info_0", 1),
    ("low_0", 1), ("high_0", 1), ("info_1", 1), ("low_1", 1), ("high_1", 0), ("conv_out", 1),
    ("centre_1", 1), ("rstd_1", 1), ("norm_1", 1), ("features_1", 1), ("query", 1), ("key", 1),
    ("value", 0), ("key_value", 0), ("denominator", 1), ("numerator", 0), ("attended", 0),
    ("message", 1), ("rstd_2", 1), ("norm_2", 0), ("features_2", 1), ("hidden_0", 0), ("hidden_1", 0),
    ("hidden_out", 0), ("tokens_3", 1), ("rstd_3", 1), ("norm_3", 1), ("features_3", 1), ("centre_4", 1),
    ("rstd_4", 1), ("norm_4", 1), ("features_4", 1), ("gates", 1), ("gate_exp", 1), ("finish_0", 0),
    ("choose_1", 1), ("choose_2", 1), ("gate_rows", 1), ("first_unit", 0), ("finish_1", 0),
]
assert sum(n for _, n in SCHEDULE) == US


def build(nc, x, wpack, w1e, reps, out):
    xd = x.rearrange("(n two) c t -> n (two c) t", two=2)
    od = out.rearrange("(n two) c t -> n (two c) t", two=2)
    with ExitStack() as ctx:
        def sb(name, shape, dt=F32):
            return ctx.enter_context(nc.sbuf_tensor(name, shape, dt))

        def sem(name):
            return ctx.enter_context(nc.semaphore(name))

        def sems(name):
            return [sem(f"{name}{g}") for g in range(G)]

        W = sb("W", [P, NW])
        X = sb("X", [P, G, T])
        XB = sb("XB", [P, 2, G, T])
        XN = sb("XN", [P, G, T])
        T1 = sb("T1", [P, G, T])
        T2 = sb("T2", [P, G, T])
        BIG = sb("BIG", [P, G, 4, T])
        S = sb("S", [P, 2, G, 2, T], F32R)
        CT = sb("CT", [P, 2, G, T], F32R)
        CHL = sb("CHL", [P, G, 2, P])
        KVM = sb("KVM", [P, G, P])
        KS = sb("KS", [P, G, HEADS])
        RZ = sb("RZ", [P, G, TB, HEADS])
        SM = sb("SM", [P, 4, G, NORMS])
        H = sb("H", [P, 2, 2, CH])
        ACC = sb("ACC", [P, G, 2, T])
        TM = sb("TM", [P, 2, CH])
        CW = sb("CW", [P, 2, CH])
        WMC = sb("WMC", [P, P])
        W2C = sb("W2C", [P, C])
        W1G = sb("W1G", [P, HID])
        BH = sb("BH", [P, 1])
        BT = sb("BT", [P, 1])
        WEH = sb("WEH", [P, E, HID], F32R)
        WEL = sb("WEL", [P, E, HID], F32R)
        REP = sb("REP", [P, NREP + NSEL, P], F32R)
        ST = sb("ST", [P, G, 32])

        def psum(name, columns):
            return ctx.enter_context(nc.psum_tensor(name, [P, columns], F32))

        R = [psum(f"R{s}", T) for s in range(G)]
        HP = [psum(f"HP{e}", CH) for e in range(2)]
        YC = [psum(f"YC{k}", CH) for k in range(2)]

        def w(name, rows=slice(0, P)):
            a, n = COLS[name]
            return W[rows, a:a + n]

        def col(k, rows=slice(0, P)):
            a = COLS["cols"][0] + k
            return W[rows, a:a + 1]

        XR = XN[:, :, :].bitcast(F32R)

        def half(c):
            return slice(c * CH, (c + 1) * CH)

        def token_blocks(c):
            return slice(c * TB // NCH, (c + 1) * TB // NCH)

        def img(k):
            return slice(k * C, (k + 1) * C)

        Q = [BIG[:, s, 0, :] for s in range(G)]
        K = [BIG[:, s, 1, :] for s in range(G)]
        V = [BIG[:, s, 2:4, :].rearrange("p a t -> p (a t)")[:, 0:TB * VW].rearrange("p (j c) -> p j c", c=VW)
             for s in range(G)]
        U = [[BIG[:, s, k, :] for k in range(2)] for s in range(G)]
        HA = [[BIG[:, s, 2 + k, :] for k in range(2)] for s in range(G)]

        w_in = sem("w_in")
        ct_zero = sem("ct_zero")
        prep_split = sem("prep_split")
        prep_pe = sem("prep_pe")
        prep_done = sem("prep_done")
        x_in = sems("x_in")
        gn_part = sem("gn_part")
        gn_stat = sem("gn_stat")
        gn_dev = sem("gn_dev")
        gn_avg = sem("gn_avg")
        gn_var = sem("gn_var")
        gn_done = sem("gn_done")
        im_ps = sem("im_ps")
        im_act = sem("im_act")
        hl_high = sem("hl_high")
        hl_done = sem("hl_done")
        rep_ps = sem("rep_ps")
        ir_done = sem("ir_done")
        prod_done = sem("prod_done")
        oc_ps = sem("oc_ps")
        oc_act = sem("oc_act")
        x1_done = sem("x1_done")
        ln_ps = sem("ln_ps")
        ln_sq = sem("ln_sq")
        ln_stat = sem("ln_stat")
        ln_tok = sem("ln_tok")
        ln_back = sem("ln_back")
        xb_part = sem("xb_part")
        xs_done = sem("xs_done")
        msg_norm = sem("msg_norm")
        qk_ps = sem("qk_ps")
        qk_exp = sem("qk_exp")
        qk_min = sem("qk_min")
        qk_done = sem("qk_done")
        v_ps = sem("v_ps")
        v_done = sem("v_done")
        kv_ps = sem("kv_ps")
        kv_done = sem("kv_done")
        den_ps = sem("den_ps")
        den_eps = sem("den_eps")
        den_done = sem("den_done")
        num_ps = sem("num_ps")
        msg_done = sem("msg_done")
        att_ps = sem("att_ps")
        att_done = sem("att_done")
        u_in = sems("u_in")
        h_ps = sem("h_ps")
        h_done = sem("h_done")
        y2_ps = sem("y2_ps")
        y2_done = sem("y2_done")
        x2_done = sem("x2_done")
        xf_done = sem("xf_done")
        sp_high = sem("sp_high")
        sp_low = sem("sp_low")
        s_in = sems("s_in")
        gate_ps = sem("gate_ps")
        lg_done = sem("lg_done")
        lg_shifted = sem("lg_shifted")
        gate_exp = sem("gate_exp")
        cw_done = sem("cw_done")
        cwt_ps = sem("cwt_ps")
        cwt_done = sem("cwt_done")
        ct_in = sems("ct_in")
        l1_ps = sem("l1_ps")
        gelu_done = sem("gelu_done")
        cwb_ps = sem("cwb_ps")
        cwb_done = sem("cwb_done")
        y_ps = sem("y_ps")
        comb_done = sem("comb_done")
        acc_done = sem("acc_done")
        fin_ps = sem("fin_ps")
        fin_done = sem("fin_done")
        out_done = sems("out_done")
        ones_set = sem("ones_set")
        dve_prep = sem("dve_prep")
        chain = sem("chain")
        ct_high = sem("ct_high")


        PIECES = [(s, c) for s in range(G) for c in range(NCH)]

        def nth(n, s, c=None):
            if c is None:
                return (n - 1) * G + s + 1
            return ((n - 1) * G + s) * NCH + c + 1

        LAST = NCH - 1

        def unit(u):
            return u // CH_UNITS, u // (2 * EP) % 2, u // 2 % EP, u % 2

        ADDS = US // EP * (EP - 1)

        def adds(u):
            return u // (2 * EP) * 2 * (EP - 1) + max(u % (2 * EP) - 2, 0)

        def gt(k):
            return T1[:, :, P * k:P * k + P]

        def rows(t):
            return t.rearrange("p g (r e) -> p g r e", e=E)

        def groups(eng, run, apart=0):
            run(0, None, 0)
            run(1, 0, 1)
            with eng.Fori(0, GROUPS // 2 - 1 - apart) as i:
                run(i * 2 + 2, i * 2 + 1, 0)
                run(i * 2 + 3, i * 2 + 2, 1)
            for a in range(GROUPS - 2 * apart, GROUPS):
                run(a, a - 1, a % 2)
            run(None, GROUPS - 1, 0)

        def interleave(a, b, stages, expert):
            u = 0
            for name, units in SCHEDULE:
                if name in stages and (b if name.startswith("finish") else a) is not None:
                    stages[name]()
                for _ in range(units if b is not None else 0):
                    expert(u)
                    u += 1

        block = ctx.enter_context(nc.Block())

        @block.sync
        def _(sp):
            sp.dma_start(W[:, :], wpack).then_inc(w_in, 16)
            sp.dma_start(BIG[:, 0, 0, :], w1e).then_inc(w_in, 16)
            sp.dma_start(BIG[:, 0, 1:3, :].rearrange("p a t -> p (a t)")[:, 0:(NREP + NSEL) * P],
                         reps).then_inc(w_in, 16)
            for s in range(G):
                sp.dma_start(X[:, s, :], xd[s]).then_inc(x_in[s], 16)

            def run(a, b, par):
                def message_norm():
                    for s in range(G):
                        sp.wait_ge(msg_norm, nth(a + 1, s, LAST))
                        for k in range(2):
                            sp.dma_start(U[s][k][0:C, :], XN[img(k), s, :]).then_inc(u_in[s], 16)
                            sp.dma_start(U[s][k][C:P, :], T2[img(k), s, :]).then_inc(u_in[s], 16)

                def next_input():
                    if isinstance(a, int) and a == GROUPS - 1:
                        return
                    for s in range(G):
                        sp.wait_ge(xs_done, nth(a + 1, s))
                        sp.dma_start(X[:, s, :], xd[a * G + G + s]).then_inc(x_in[s], 16)

                def expert_input():
                    for s in range(G):
                        sp.wait_ge(sp_low, nth(a + 1, s, LAST))
                        for k in range(2):
                            sp.dma_start(S[0:C, par, s, k, :].bitcast(F32), XN[img(k), s, :])\
                                .then_inc(s_in[s], 16)
                            sp.dma_start(S[C:P, par, s, k, :].bitcast(F32), T2[img(k), s, :])\
                                .then_inc(s_in[s], 16)

                def gate_weights():
                    sp.wait_ge(cwt_done, a + 1)
                    for s in range(G):
                        for part in range(2):
                            sp.dma_start(CT[16 * part:16 * part + 16, par, s, :].bitcast(F32),
                                         CHL[:, s, part, :]).then_inc(ct_in[s], 16)

                def store(s):
                    sp.wait_ge(fin_done, (b * G + s + 1) * NCH)
                    sp.dma_start(od[b * G + s], XB[:, 1 - par, s, :]).then_inc(out_done[s], 16)

                def expert(u):
                    pass

                interleave(a, b, {"features_1": next_input, "features_2": message_norm,
                                  "features_4": expert_input, "gate_rows": gate_weights, "finish_0": lambda: store(0),
                                  "finish_1": lambda: store(1)}, expert)

            groups(sp, run, apart=1)
            for s in range(G):
                sp.wait_ge(out_done[s], GROUPS * 16)

        @block.tensor
        def _(pe):
            mm = nc.tensor.matmul

            pe.wait_ge(w_in, 48)
            mm(R[0][:, 0:P], w("wm_t"), w("center"), start=True, stop=True)
            mm(R[0][:, CH:CH + C], w("w2_t"), w("center")[:, 0:C], start=True, stop=True)
            mm(R[1][:, 0:1], w("w1"), col(B1), start=True, stop=True).then_inc(prep_pe, 1)
            pe.wait_ge(prep_done, 1)

            def run(a, b, par):
                def group_stats():
                    for s in range(G):
                        pe.wait_ge(gn_stat, nth(a + 1, s))
                        mm(R[s][:, 0:2], w("pairavg"), ST[:, s, 12:14], start=True, stop=True).then_inc(gn_avg, 1)

                def info_mask():
                    for s, c in PIECES:
                        pe.wait_ge(gn_done, nth(a + 1, s))
                        mm(R[s][0:C, half(c)], w("wim"), XN[:, s, half(c)], start=True, stop=True).then_inc(im_ps, 1)

                def replicate(n):
                    for s, c in PIECES:
                        if n == 0:
                            pe.wait_ge(hl_done, nth(a + 1, s, c))
                        elif n % 3 == 1:
                            pe.wait_ge(ir_done, nth(a * 2 + n // 3 + 1, s, c))
                        else:
                            pe.wait_ge(prod_done, nth(a * 4 + (n + 1) // 3 + n // 3, s, c))
                        mm(R[s][:, half(c)], REP[:, n, :], S[:, par, s, 0, half(c)], start=True, stop=True).then_inc(rep_ps, 1)

                def conv_out():
                    for s, c in PIECES:
                        pe.wait_ge(prod_done, nth(a * 4 + 4, s, c))
                        for h in range(2):
                            for k in range(2):
                                last = mm(R[s][img(k), half(c)], w("ow")[:, C * h:C * h + C],
                                          BIG[:, s, 2 * k + h, half(c)], start=(h == 0), stop=(h == 1))
                        last.then_inc(oc_ps, 1)

                def blocks(c):
                    return range(c * TB // NCH, (c + 1) * TB // NCH)

                def tokens(s, c, src):
                    for j in blocks(c):
                        last = nc.tensor.transpose(R[s][:, P * j:P * j + P], src[:, s, P * j:P * j + P], w("ident"))
                    return last

                def centre_1():
                    for s, c in PIECES:
                        pe.wait_ge(x1_done, nth(a + 1, s, c))
                        by_token(s, c, X, w("center")).then_inc(ln_ps, 1)

                def features(k):
                    for s, c in PIECES:
                        pe.wait_ge(ln_tok, nth(a * LNS + k, s, c))
                        tokens(s, c, T1).then_inc(ln_back, 1)

                def query():
                    for s, c in PIECES:
                        pe.wait_ge(xb_part, nth(a + 1, s, c))
                        mm(R[s][:, half(c)], w("wq"), XN[:, s, half(c)], start=True, stop=True).then_inc(qk_ps, 1)

                def by_token(s, c, src, weights):
                    for j in blocks(c):
                        last = mm(R[s][:, P * j:P * j + P], src[:, s, P * j:P * j + P], weights,
                                  start=True, stop=True)
                    return last

                def key():
                    for s, c in PIECES:
                        pe.wait_ge(qk_done, nth(a * 2 + 1, s, c))
                        by_token(s, c, XN, w("wk")).then_inc(qk_ps, 1)

                def value():
                    for s, c in PIECES:
                        pe.wait_ge(qk_done, nth(a * 2 + 2, s, c))
                        by_token(s, c, XN, w("wv")).then_inc(v_ps, 1)

                def key_value():
                    for s in range(G):
                        pe.wait_ge(v_done, nth(a + 1, s, LAST))
                        pe.wait_ge(ones_set, nth(a + 1, s))
                        for j in range(TB):
                            last = mm(R[s][:, 0:VW], K[s][:, P * j:P * j + P], V[s][:, j, :],
                                      start=(j == 0), stop=(j == TB - 1))
                        last.then_inc(kv_ps, 1)

                def denominator():
                    for s in range(G):
                        pe.wait_ge(kv_done, nth(a + 1, s))
                        for j in range(TB):
                            last = mm(R[s][:, HEADS * j:HEADS * j + HEADS], Q[s][:, P * j:P * j + P], KS[:, s, :],
                                      start=True, stop=True)
                        last.then_inc(den_ps, 1)

                def numerator():
                    for s, c in PIECES:
                        if c == 0:
                            pe.wait_ge(den_eps, nth(a + 1, s))
                        for j in blocks(c):
                            last = mm(R[s][:, P * j:P * j + P], Q[s][:, P * j:P * j + P], KVM[:, s, :],
                                      start=True, stop=True)
                        last.then_inc(num_ps, 1)

                def attended():
                    for s, c in PIECES:
                        pe.wait_ge(msg_done, nth(a + 1, s, c))
                        tokens(s, c, T2).then_inc(att_ps, 1)

                def message():
                    for s, c in PIECES:
                        pe.wait_ge(att_done, nth(a + 1, s, c))
                        by_token(s, c, T1, WMC[:, :]).then_inc(ln_ps, 1)

                def hidden(k):
                    for s, c in PIECES:
                        if k == 0:
                            pe.wait_ge(u_in[s], a * 64 + 64)
                        else:
                            pe.wait_ge(h_done, nth(a * 2 + 1, s, c))
                        mm(R[s][:, half(c)], W1G[:, :], U[s][k][:, half(c)], start=True, stop=True)\
                            .then_inc(h_ps, 1)

                def hidden_out():
                    for s, c in PIECES:
                        pe.wait_ge(h_done, nth(a * 2 + 2, s, c))
                        for k in range(2):
                            last = mm(R[s][img(k), half(c)], W2C[:, :], HA[s][k][:, half(c)],
                                      start=True, stop=True)
                        last.then_inc(y2_ps, 1)

                def tokens_3():
                    for s, c in PIECES:
                        pe.wait_ge(y2_done, nth(a + 1, s, c))
                        tokens(s, c, T1).then_inc(ln_ps, 1)

                def centre_4():
                    for s, c in PIECES:
                        pe.wait_ge(x2_done, nth(a + 1, s, c))
                        by_token(s, c, XB[:, par, :, :], w("center")).then_inc(ln_ps, 1)

                def gates():
                    for s, c in PIECES:
                        pe.wait_ge(xf_done, nth(a + 1, s, c))
                        for j in blocks(c):
                            last = mm(R[s][:, 2 * E * j:2 * E * (j + 1)], T1[:, s, P * j:P * j + P], w("gw"),
                                      start=True, stop=True)
                        if c == LAST:
                            last.then_inc(gate_ps, 1)

                def gate_rows():
                    pe.wait_ge(cw_done, a + 1)
                    for s in range(G):
                        last = nc.tensor.transpose(R[s][:, 0:P], T1[:, s, 0:P], w("ident"))
                    last.then_inc(cwt_ps, 1)

                def hidden_layers(g, p, u):
                    s, k, ep, c = unit(u)
                    if u % CH_UNITS == 0:
                        pe.wait_ge(s_in[s], g * 64 + 64)
                    for e in range(2):
                        ex = 2 * ep + e
                        mm(HP[e][:, :], WEH[:, ex, :], S[:, p, s, k, half(c)], start=True, stop=False)
                        mm(HP[e][:, :], WEL[:, ex, :], S[:, p, s, k, half(c)], start=False, stop=True)\
                            .then_inc(l1_ps, 1)

                def gate_weights(u):
                    s, k, ep, c = unit(u)
                    if u % CH_UNITS == 0:
                        pe.wait_ge(ct_in[s], b * 32 + 32)
                    if u >= 2 or not (isinstance(b, int) and b == 0):
                        pe.wait_ge(comb_done, b * US + u - 1)
                    mm(YC[u % 2][:, :], REP[:, NREP + k * EP + ep, :], CT[:, 1 - par, s, half(c)],
                       start=True, stop=True).then_inc(cwb_ps, 1)

                def expert(u):
                    s, k, ep, c = unit(u)
                    if u == 0:
                        gate_weights(0)
                    pe.wait_ge(gelu_done, (b * US + u + 1) * 2)
                    if u + 1 < US:
                        hidden_layers(b, 1 - par, u + 1)
                        gate_weights(u + 1)
                    pe.wait_ge(cwb_done, b * US + u + 1)
                    for e in range(2):
                        ex = 2 * ep + e
                        last = mm(YC[u % 2][img(e), :], w("w2e")[:, C * ex:C * ex + C], H[:, u % 2, e, :],
                                  start=True, stop=True)
                    last.then_inc(y_ps, 1)

                def finish(s):
                    pe.wait_ge(comb_done, b * US + (s + 1) * CH_UNITS)
                    pe.wait_ge(acc_done, b * ADDS + adds((s + 1) * CH_UNITS))
                    if a is not None and s == 0:
                        pe.wait_ge(xf_done, nth(a + 1, G - 1, LAST))
                    for c in range(NCH):
                        if s:
                            pe.wait_ge(fin_done, b * G * NCH + c + 1)
                        for k in range(2):
                            last = mm(R[c][img(k), CH:T], w("fold"), ACC[:, s, k, half(c)], start=True, stop=True)
                        last.then_inc(fin_ps, 1)

                interleave(a, b, {
                    "group_stats": group_stats, "info_mask": info_mask,
                    "info_0": lambda: replicate(0), "low_0": lambda: replicate(1),
                    "high_0": lambda: replicate(2), "info_1": lambda: replicate(3),
                    "low_1": lambda: replicate(4), "high_1": lambda: replicate(5),
                    "conv_out": conv_out, "centre_1": centre_1,
                    "features_1": lambda: features(1),
                    "query": query, "key": key, "value": value, "key_value": key_value,
                    "denominator": denominator, "numerator": numerator, "attended": attended,
                    "message": message, "features_2": lambda: features(2),
                    "hidden_0": lambda: hidden(0), "hidden_1": lambda: hidden(1),
                    "hidden_out": hidden_out, "tokens_3": tokens_3,
                    "features_3": lambda: features(3), "centre_4": centre_4,
                    "features_4": lambda: features(4), "gates": gates, "gate_rows": gate_rows,
                    "first_unit": lambda: hidden_layers(a, par, 0),
                    "finish_0": lambda: finish(0), "finish_1": lambda: finish(1),
                }, expert)

            groups(pe, run)

        @block.scalar
        def _(act):
            f = nc.scalar.activation
            act.wait_ge(w_in, 48)
            f(BT[:, :], col(B_IM), ACT.Copy, scale=0.5).then_inc(prep_split, 1)
            act.wait_ge(prep_done, 1)
            act.wait_ge(prep_split, 1)

            def run(a, b, par):
                first = b is None or (isinstance(b, int) and b == 0)

                def info_mask():
                    for s, c in PIECES:
                        act.wait_ge(im_ps, nth(a + 1, s, c))
                        f(T1[0:32, s, half(c)], R[s][0:32, half(c)], ACT.Relu, bias=col(B_IM, slice(0, 32)))
                        f(T1[32:64, s, half(c)], R[s][32:64, half(c)], ACT.Tanh, bias=BT[32:64, :], scale=0.5)\
                            .then_inc(im_act, 1)

                def info(k):
                    for s, c in PIECES:
                        act.wait_ge(rep_ps, nth(a * NREP + 3 * k + 1, s, c))
                        f(T2[:, s, half(c)], R[s][:, half(c)], ACT.Copy).then_inc(ir_done, 1)

                def conv_out():
                    for s, c in PIECES:
                        act.wait_ge(oc_ps, nth(a + 1, s, c))
                        f(T1[:, s, half(c)], R[s][:, half(c)], ACT.Relu, bias=col(B_OUT), scale=0.5).then_inc(oc_act, 1)

                def square(k):
                    for s, c in PIECES:
                        act.wait_ge(ln_ps, nth(a * LNS + k, s, c))
                        f(T2[:, s, half(c)], R[s][:, half(c)], ACT.Square).then_inc(ln_sq, 1)

                def features_1():
                    for s, c in PIECES:
                        act.wait_ge(ln_back, nth(a * LNS + 1, s, c))
                        f(XN[:, s, half(c)], R[s][:, half(c)], ACT.Copy)
                        if c == 0 and not first:
                            act.wait_ge(out_done[s], b * 16)
                        f(XB[:, par, s, half(c)], R[s][:, half(c)], ACT.Identity, bias=col(B2)).then_inc(xb_part, 1)

                def features_4():
                    copy_out(ln_back, a * LNS + 4, T1, xf_done)
                    for s, c in PIECES:
                        act.wait_ge(xf_done, nth(a + 1, s, c))
                        f(XR[:, s, half(c)], T1[:, s, half(c)], ACT.Copy).then_inc(sp_high, 1)

                def copy_out(ready, n, dst, done):
                    for s, c in PIECES:
                        act.wait_ge(ready, nth(n, s, c))
                        f(dst[:, s, half(c)], R[s][:, half(c)], ACT.Copy).then_inc(done, 1)

                def exponential(n):
                    for s, c in PIECES:
                        act.wait_ge(qk_ps, nth(a * 2 + n, s, c))
                        f(T1[:, s, half(c)], R[s][:, half(c)], ACT.Exp).then_inc(qk_exp, 1)

                def value():
                    for s, c in PIECES:
                        act.wait_ge(v_ps, nth(a + 1, s, c))
                        f(V[s][:, token_blocks(c), 0:P], R[s][:, half(c)].rearrange("p (j c) -> p j c", c=P),
                          ACT.Copy).then_inc(v_done, 1)

                def hidden(k):
                    for s, c in PIECES:
                        act.wait_ge(h_ps, nth(a * 2 + k + 1, s, c))
                        f(HA[s][k][:, half(c)], R[s][:, half(c)], ACT.Relu, bias=BH[:, :]).then_inc(h_done, 1)

                def exponential_of_gates():
                    act.wait_ge(lg_shifted, a + 1)
                    f(gt(1), gt(0), ACT.Exp).then_inc(gate_exp, 1)

                def gelu(g, u):
                    ep = unit(u)[2]
                    for e in range(2):
                        act.wait_ge(l1_ps, (g * US + u) * 2 + e + 1)
                        f(H[:, u % 2, e, :], HP[e][:, :], ACT.Gelu, bias=col(B1E + 2 * ep + e))\
                            .then_inc(gelu_done, 1)

                def gate_weights(u):
                    if u >= 2 or not (isinstance(b, int) and b == 0):
                        act.wait_ge(comb_done, b * US + u - 1)
                    act.wait_ge(cwb_ps, b * US + u + 1)
                    f(CW[:, u % 2, :], YC[u % 2][:, :], ACT.Copy).then_inc(cwb_done, 1)

                def expert(u):
                    if u == 0:
                        gate_weights(0)
                    if u + 1 < US:
                        gelu(b, u + 1)
                        gate_weights(u + 1)

                interleave(a, b, {
                    "info_mask": info_mask, "info_0": lambda: info(0), "info_1": lambda: info(1),
                    "conv_out": conv_out, "centre_1": lambda: square(1), "features_1": features_1,
                    "query": lambda: exponential(1), "key": lambda: exponential(2), "value": value,
                    "attended": lambda: copy_out(att_ps, a + 1, T1, att_done),
                    "message": lambda: square(2),
                    "features_2": lambda: copy_out(ln_back, a * LNS + 2, T2, msg_norm),
                    "hidden_0": lambda: hidden(0), "hidden_1": lambda: hidden(1),
                    "hidden_out": lambda: copy_out(y2_ps, a + 1, T1, y2_done),
                    "tokens_3": lambda: square(3), "centre_4": lambda: square(4),
                    "features_4": features_4,
                    "gate_exp": exponential_of_gates, "first_unit": lambda: gelu(a, 0),
                }, expert)

            groups(act, run)

        @block.gpsimd
        def _(pool):
            nc.gpsimd.memset(CT[:, :, :, :].bitcast(F32), 0.0).then_inc(ct_zero, 1)

            def run(a, b, par):
                def residual():
                    for s in range(G):
                        pool.wait_ge(xb_part, nth(a + 1, s, LAST))
                        nc.gpsimd.tensor_tensor(XB[:, par, s, :], XB[:, par, s, :], X[:, s, :], ALU.add)\
                            .then_inc(xs_done, 1)

                def expert(u):
                    s, k, ep, c = unit(u)
                    if ep:
                        pool.wait_ge(comb_done, b * US + u + 1)
                        acc = ACC[:, s, k, half(c)]
                        nc.gpsimd.tensor_tensor(acc, TM[:, u % 2, :], acc, ALU.add).then_inc(acc_done, 1)

                interleave(a, b, {"features_1": residual}, expert)

            groups(pool, run)

        @block.vector
        def _(dve):
            v = nc.vector

            dve.wait_ge(w_in, 48)
            raw = BIG[:, 0, 0, :].rearrange("p (e h) -> p e h", h=HID)
            v.tensor_copy(WEH[:, :, :], raw).then_inc(dve_prep, 1)
            v.tensor_copy(REP[:, :, :], BIG[:, 0, 1:3, :].rearrange("p a t -> p (a t)")
                          [:, 0:(NREP + NSEL) * P].rearrange("p (n c) -> p n c", c=P)).then_inc(dve_prep, 1)
            dve.wait_ge(dve_prep, 1)
            v.tensor_tensor(WEL[:, :, :], raw, WEH[:, :, :].bitcast(F32), ALU.subtract).then_inc(dve_prep, 1)
            v.tensor_scalar(W1G[:, :], w("w1"), col(G1), None, ALU.mult).then_inc(dve_prep, 1)
            dve.wait_ge(prep_pe, 1)
            v.tensor_copy(WMC[:, :], R[0][:, 0:P]).then_inc(dve_prep, 1)
            v.tensor_copy(W2C[:, :], R[0][:, CH:CH + C]).then_inc(dve_prep, 1)
            v.tensor_copy(BH[:, :], R[1][:, 0:1]).then_inc(dve_prep, 1)
            dve.wait_ge(dve_prep, 7)
            dve.wait_ge(ct_zero, 1)
            v.memset(ST[:, 0, 30:31], 0.0).then_inc(prep_done, 1)

            chain_steps = [0]

            def run(a, b, par):
                steps = [0]

                def link(ins):
                    steps[0] += 1
                    ins.then_inc(chain, 1)
                    dve.wait_ge(chain, a * chain_steps[0] + steps[0])

                def rsqrt(n):
                    hz, t, y = (SM[:, k, :, 0:n] for k in (1, 2, 3))
                    link(v.tensor_scalar(y.bitcast(I32), hz.bitcast(I32), -0.5, RSQRT_GUESS, ALU.mult, ALU.add))
                    for _ in range(3):
                        link(v.tensor_tensor(t, y, y, ALU.mult))
                        link(v.tensor_tensor(t, t, hz, ALU.mult))
                        link(v.scalar_tensor_tensor(out=y, in0=t, scalar=-1.5, in1=y, op0=ALU.add, op1=ALU.mult))

                def channel_stats():
                    for s in range(G):
                        dve.wait_ge(x_in[s], a * 16 + 16)
                        for c in range(NCH):
                            ins = v.bn_stats(ST[:, s, 6 * c:6 * c + 6], X[:, s, half(c)])
                        ins.then_inc(gn_part, 1)
                    for s in range(G):
                        dve.wait_ge(gn_part, nth(a + 1, s))
                        v.memset(ST[:, s, 31:32], 0.0)
                        v.bn_aggr(ST[:, s, 12:14], ST[:, s, 0:12]).then_inc(gn_stat, 1)

                def group_stats():
                    for s in range(G):
                        dve.wait_ge(gn_avg, nth(a + 1, s))
                        dve.wait_ge(gn_stat, nth(a + 1, s))
                        v.tensor_tensor(ST[:, s, 14:15], ST[:, s, 12:13], R[s][:, 0:1], ALU.subtract)\
                            .then_inc(gn_dev, 1)
                    for s in range(G):
                        dve.wait_ge(gn_dev, nth(a + 1, s))
                        v.scalar_tensor_tensor(out=SM[:, 0, s, 0:1], in0=ST[:, s, 14:15], scalar=ST[:, s, 14:15],
                                               in1=R[s][:, 1:2], op0=ALU.mult, op1=ALU.add).then_inc(gn_var, 1)
                    dve.wait_ge(gn_var, nth(a + 1, G - 1))
                    link(v.tensor_scalar(SM[:, 1, :, 0:1], SM[:, 0, :, 0:1], LN_EPS, 0.5, ALU.add, ALU.mult))
                    rsqrt(1)

                def group_norm():
                    for s in range(G):
                        v.tensor_scalar(XN[:, s, :], X[:, s, :], R[s][:, 0:1], SM[:, 3, s, 0:1],
                                        ALU.subtract, ALU.mult).then_inc(gn_done, 1)

                def info_mask():
                    for s, c in PIECES:
                        dve.wait_ge(im_act, nth(a + 1, s, c))
                        high = S[0:C, par, s, 0, half(c)]
                        v.tensor_copy(high, T1[0:C, s, half(c)]).then_inc(hl_high, 1)
                        dve.wait_ge(hl_high, nth(a + 1, s, c))
                        v.tensor_tensor(S[C:P, par, s, 0, half(c)], T1[0:C, s, half(c)], high.bitcast(F32),
                                        ALU.subtract).then_inc(hl_done, 1)

                def product(k, h):
                    for s, c in PIECES:
                        if h == 0:
                            dve.wait_ge(ir_done, nth(a * 2 + k + 1, s, c))
                        dve.wait_ge(rep_ps, nth(a * NREP + 3 * k + h + 2, s, c))
                        v.scalar_tensor_tensor(out=BIG[:, s, 2 * k + h, half(c)], in0=R[s][:, half(c)], scalar=1.0,
                                               in1=T2[:, s, half(c)], op0=ALU.add, op1=ALU.mult)\
                            .then_inc(prod_done, 1)

                def conv_out():
                    for s, c in PIECES:
                        dve.wait_ge(oc_act, nth(a + 1, s, c))
                        v.tensor_tensor(X[:, s, half(c)], X[:, s, half(c)], T1[:, s, half(c)], ALU.add)\
                            .then_inc(x1_done, 1)
                        if c == LAST:
                            v.memset(V[s][:, :, P:VW], 1.0).then_inc(ones_set, 1)

                def norms(t):
                    return t.rearrange("p (n c) -> p n c", c=C)

                def some_norms(c):
                    return slice(c * NORMS // NCH, (c + 1) * NORMS // NCH)

                def squares(k):
                    for s, c in PIECES:
                        dve.wait_ge(ln_sq, nth(a * LNS + k, s, c))
                        v.reduce_sum(SM[:, 0, s, some_norms(c)], norms(T2[:, s, half(c)]), AX_X).then_inc(ln_stat, 1)

                def rstd(k):
                    dve.wait_ge(ln_stat, nth(a * LNS + k, G - 1, LAST))
                    link(v.tensor_scalar(SM[:, 1, :, :], SM[:, 0, :, :], 0.5 / C, 0.5 * LN_EPS,
                                         ALU.mult, ALU.add))
                    rsqrt(NORMS)
                    scale(0)

                def scale(s):
                    for c in range(NCH):
                        v.tensor_tensor(norms(T1[:, s, half(c)]), norms(R[s][:, half(c)]),
                                        SM[:, 3, s, some_norms(c)].unsqueeze(2)
                                        .broadcast_to([P, NORMS // NCH, C]), ALU.mult).then_inc(ln_tok, 1)

                def elu_plus_one(n, dst):
                    for s, c in PIECES:
                        dve.wait_ge(qk_exp, nth(a * 2 + n, s, c))
                        v.tensor_scalar(T1[:, s, half(c)], T1[:, s, half(c)], 1.0, None, ALU.min).then_inc(qk_min, 1)
                    for s, c in PIECES:
                        dve.wait_ge(qk_min, nth(a * 2 + n, s, c))
                        v.scalar_tensor_tensor(out=dst[s][:, half(c)], in0=R[s][:, half(c)], scalar=0.0, in1=T1[:, s, half(c)],
                                               op0=ALU.max, op1=ALU.add).then_inc(qk_done, 1)

                def key_value():
                    for s in range(G):
                        dve.wait_ge(kv_ps, nth(a + 1, s))
                        v.tensor_tensor(KVM[:, s, :], R[s][:, 0:P], w("headmask"), ALU.mult)
                        v.tensor_scalar(KS[:, s, :], w("headmask").rearrange("p (h d) -> p h d", d=HD)[:, :, 0],
                                        R[s][:, P:P + 1], None, ALU.mult)\
                            .then_inc(kv_done, 1)

                def denominator():
                    for s in range(G):
                        dve.wait_ge(den_ps, nth(a + 1, s))
                        v.tensor_scalar(RZ[:, s, :, :], R[s][:, 0:TB * HEADS].rearrange("p (j h) -> p j h", h=HEADS),
                                        ATT_EPS, None, ALU.add).then_inc(den_eps, 1)
                    for s in range(G):
                        dve.wait_ge(den_eps, nth(a + 1, s))
                        v.reciprocal(RZ[:, s, :, :], RZ[:, s, :, :]).then_inc(den_done, 1)

                def numerator():
                    for s, c in PIECES:
                        if c == 0:
                            dve.wait_ge(den_done, nth(a + 1, s))
                        dve.wait_ge(num_ps, nth(a + 1, s, c))
                        v.tensor_tensor(T2[:, s, half(c)].rearrange("p (h d) -> p h d", d=HD),
                                        R[s][:, half(c)].rearrange("p (h d) -> p h d", d=HD),
                                        RZ[:, s, token_blocks(c), :].rearrange("p j h -> p (j h)").unsqueeze(2)
                                        .broadcast_to([P, TB * HEADS // NCH, HD]), ALU.mult).then_inc(msg_done, 1)

                def features_3():
                    for s, c in PIECES:
                        if c == 0:
                            dve.wait_ge(xs_done, nth(a + 1, s))
                        dve.wait_ge(ln_back, nth(a * LNS + 3, s, c))
                        v.scalar_tensor_tensor(out=XB[:, par, s, half(c)], in0=R[s][:, half(c)], scalar=col(G2),
                                               in1=XB[:, par, s, half(c)], op0=ALU.mult, op1=ALU.add)\
                            .then_inc(x2_done, 1)

                def features_4():
                    for s, c in PIECES:
                        dve.wait_ge(sp_high, nth(a + 1, s, c))
                        v.tensor_tensor(T2[:, s, half(c)], T1[:, s, half(c)], XN[:, s, half(c)], ALU.subtract)\
                            .then_inc(sp_low, 1)

                best = T1[:, :, 6 * P:6 * P + 2 * TB]
                def per_token(t):
                    return t.unsqueeze(3).broadcast_to([P, G, 2 * TB, E])

                def first_largest(values, chosen):
                    link(v.scalar_tensor_tensor(out=chosen, in0=values, scalar=0.0, op0=ALU.is_equal, op1=ALU.mult,
                                                in1=w("rank").unsqueeze(1).broadcast_to([P, G, P])))
                    link(v.reduce_max(best, rows(chosen), AX_X))
                    link(v.tensor_tensor(rows(chosen), rows(chosen), per_token(best), ALU.is_equal))

                def below_largest(t):
                    link(v.reduce_max(best, rows(t), AX_X))
                    return v.tensor_tensor(rows(t), rows(t), per_token(best), ALU.subtract)

                def gates():
                    dve.wait_ge(sp_low, nth(a + 1, G - 1, LAST))
                    for s in range(G):
                        dve.wait_ge(gate_ps, nth(a + 1, s))
                        v.tensor_tensor(T1[:, s, 0:P], R[s][:, 0:P], w("gb"), ALU.add).then_inc(lg_done, 1)
                    dve.wait_ge(lg_done, nth(a + 1, G - 1))
                    below_largest(gt(0)).then_inc(lg_shifted, 1)

                def choose_1():
                    dve.wait_ge(lg_shifted, a + 1)
                    first_largest(gt(0), gt(2))
                    link(v.scalar_tensor_tensor(out=gt(3), in0=gt(2), scalar=-FAR, in1=gt(0),
                                                op0=ALU.mult, op1=ALU.add))

                def choose_2():
                    link(below_largest(gt(3)))
                    first_largest(gt(3), gt(4))
                    link(v.tensor_tensor(gt(2), gt(2), gt(4), ALU.add))
                    dve.wait_ge(gate_exp, a + 1)
                    link(v.tensor_tensor(gt(2), gt(2), gt(1), ALU.mult))
                    link(v.reduce_sum(best, rows(gt(1)), AX_X))
                    link(v.reciprocal(best, best))
                    for s in range(G):
                        for k in range(2):
                            ins = v.tensor_tensor(
                                T1[:, s, k * C:k * C + C].rearrange("p (e j) -> p j e", e=E),
                                T1[:, s, 2 * P:3 * P].rearrange("p (j k e) -> p j k e", k=2, e=E)[:, :, k, :],
                                best[:, s, :].rearrange("p (j k) -> p j k", k=2)[:, :, k].unsqueeze(2)
                                .broadcast_to([P, TB, E]), ALU.mult)
                    ins.then_inc(cw_done, 1)

                def gate_rows():
                    chain_steps[0] = steps[0]
                    dve.wait_ge(cwt_ps, a + 1)
                    for s in range(G):
                        ins = v.tensor_copy(CHL[:, s, 0, :].bitcast(F32R), R[s][:, 0:P])
                    ins.then_inc(ct_high, 1)
                    dve.wait_ge(ct_high, a + 1)
                    for s in range(G):
                        ins = v.tensor_tensor(CHL[:, s, 1, :], R[s][:, 0:P], CHL[:, s, 0, :], ALU.subtract)
                    ins.then_inc(cwt_done, 1)

                def expert(u):
                    s, k, ep, c = unit(u)
                    if ep and adds(u - 1):
                        dve.wait_ge(acc_done, b * ADDS + adds(u - 1))
                    dve.wait_ge(y_ps, b * US + u + 1)
                    dve.wait_ge(cwb_done, b * US + u + 1)
                    dst = TM[:, u % 2, :] if ep else ACC[:, s, k, half(c)]
                    v.scalar_tensor_tensor(out=dst, in0=YC[u % 2][:, :], scalar=col(B2E + ep), in1=CW[:, u % 2, :],
                                           op0=ALU.add, op1=ALU.mult).then_inc(comb_done, 1)

                def finish(s):
                    for c in range(NCH):
                        dve.wait_ge(fin_ps, (b * G + s) * NCH + c + 1)
                        x = XB[:, 1 - par, s, half(c)]
                        v.tensor_tensor(x, R[c][:, CH:T], x, ALU.add).then_inc(fin_done, 1)

                interleave(a, b, {
                    "channel_stats": channel_stats, "group_stats": group_stats, "group_norm": group_norm,
                    "info_mask": info_mask,
                    "low_0": lambda: product(0, 0), "high_0": lambda: product(0, 1),
                    "low_1": lambda: product(1, 0), "high_1": lambda: product(1, 1),
                    "conv_out": conv_out,
                    "centre_1": lambda: squares(1), "rstd_1": lambda: rstd(1), "norm_1": lambda: scale(1),
                    "query": lambda: elu_plus_one(1, Q), "key": lambda: elu_plus_one(2, K),
                    "key_value": key_value, "denominator": denominator, "numerator": numerator,
                    "message": lambda: squares(2), "rstd_2": lambda: rstd(2), "norm_2": lambda: scale(1),
                    "tokens_3": lambda: squares(3), "rstd_3": lambda: rstd(3), "norm_3": lambda: scale(1),
                    "features_3": features_3,
                    "centre_4": lambda: squares(4), "rstd_4": lambda: rstd(4), "norm_4": lambda: scale(1),
                    "features_4": features_4, "gates": gates,
                    "choose_1": choose_1, "choose_2": choose_2, "gate_rows": gate_rows,
                    "finish_0": lambda: finish(0), "finish_1": lambda: finish(1),
                }, expert)

            groups(dve, run)


def kernel(**inputs):
    import concourse.bacc as bacc
    from concourse.bass_utils import run_bass_kernel_spmd

    f = lambda n: np.asarray(inputs[n])
    wp = np.zeros((P, NW), np.float32)

    def put(name, a, rows=0, at=0):
        a = np.atleast_2d(a)
        c = COLS[name][0] + at
        wp[rows:rows + a.shape[0], c:c + a.shape[1]] = a

    info, mask, ow = f("L0_conv_info_w"), f("L0_conv_mask_w"), f("L0_conv_out_w")
    wm, w1, w2 = f("L1_attn_Wm"), f("L1_attn_W1"), f("L1_attn_W2")
    centre = np.eye(C, dtype=np.float32) - np.float32(1 / C)
    for k in range(2):
        r = k * C
        put("wim", info.T, r, IC * k)
        put("wim", mask.T, r, 2 * IC + IC * k)
        put("center", centre, r, r)
        put("mean", np.full((C, C), 1 / C, np.float32), r, r)
        put("wq", f("L1_attn_Wq"), r, r)
        put("wk", f("L1_attn_Wk"), r, r)
        put("wv", f("L1_attn_Wv"), r, r)
        put("wm_t", wm.T, r, r)
        put("gw", f("L1_ffn_gate_w"), r, E * k)
        put("fold", np.eye(C, dtype=np.float32), r)
        put("cols", f("L0_conv_info_b")[:, None], IC * k, B_IM)
        put("cols", f("L0_conv_mask_b")[:, None], 2 * IC + IC * k, B_IM)
        put("cols", f("L0_conv_out_b")[:, None], r, B_OUT)
        put("cols", f("L1_attn_g2")[:, None], r, G2)
        put("cols", f("L1_attn_b2")[:, None], r, B2)
    for h in range(2):
        put("ow", ow.T[P * h:P * h + P], 0, C * h)
    put("w1", w1)
    put("w2_t", w2.T)
    put("headmask", np.kron(np.eye(P // HD), np.ones((HD, HD))).astype(np.float32))
    put("pairavg", np.kron(np.eye(C), np.full((2, 2), 0.5)).astype(np.float32))
    put("ident", np.eye(P, dtype=np.float32))
    put("cols", np.ones((C, 1), np.float32), 0, G1)
    put("cols", f("L1_attn_g1")[:, None], C, G1)
    put("cols", f("L1_attn_b1")[:, None], C, B1)
    put("gb", np.broadcast_to(np.tile(f("L1_ffn_gate_b"), 2 * TB), (P, 2 * TB * E)))
    put("rank", np.broadcast_to(np.tile(np.arange(E, 0, -1, dtype=np.float32), 2 * TB), (P, 2 * TB * E)))
    we1, we2 = f("L1_ffn_W1"), f("L1_ffn_W2")
    for e in range(E):
        put("w2e", we2[e], 0, C * e)
        put("cols", f("L1_ffn_b1")[e][:, None], 0, B1E + e)
        put("cols", f("L1_ffn_b2")[e][:, None], C * (e % 2), B2E + e // 2)
    w1e = np.concatenate([we1.transpose(1, 0, 2).reshape(C, E * HID)] * 2, axis=0)
    reps = np.zeros((P, NREP + NSEL, P), np.float32)
    for k in range(2):
        for part in range(2):
            for o in range(P):
                reps[C * part + IC * k + o % IC, 3 * k, o] = 1
                for h in range(2):
                    reps[C * part + 2 * IC + IC * k + o // IC + HD * h, 3 * k + 1 + h, o] = 1
                for ep in range(EP):
                    reps[16 * part + E * k + 2 * ep + o // C, NREP + EP * k + ep, o] = 1

    nc = bacc.Bacc("TRN2", target_bir_lowering=False, num_devices=1)
    xs = f("x")
    arrays = {"x": np.ascontiguousarray(xs.reshape(IMGS, C, T)), "wpack": wp,
              "w1e": np.ascontiguousarray(w1e), "reps": reps.reshape(P, -1)}
    aps = [nc.dram_tensor(n, a.shape, F32, kind="ExternalInput").ap() for n, a in arrays.items()]
    out = nc.dram_tensor("out", (IMGS, C, T), F32, kind="ExternalOutput").ap()
    build(nc, *aps, out)
    r = run_bass_kernel_spmd(nc, [arrays], core_ids=[0])
    return r.results[0]["out"].reshape(xs.shape)
```

```python
from contextlib import ExitStack

import numpy as np

import concourse.bass as bass
from concourse import mybir

F32 = mybir.dt.float32
F32R = mybir.dt.float32r
I32 = mybir.dt.int32
ALU = mybir.AluOpType
ACT = mybir.ActivationFunctionType
AX_X = mybir.AxisListType.X

P = 128
C = 64
IMGS = 32
T = 1024
PAIRS = IMGS // 2
G = 2
GROUPS = PAIRS // G
CH = 512
NCH = T // CH
TB = T // P
IC = 16
E = 8
HD = 8
HID = 128
EP = E // 2
CH_UNITS = 2 * EP * 2
US = G * CH_UNITS
VW = P + 2
LN_EPS = 1e-5
ATT_EPS = 1e-6
LNS = 4

COLS = {}
_at = 0
for _name, _width in [
    ("wim", 64), ("ow", 2 * C), ("center", P), ("wq", P), ("wk", P), ("wv", P),
    ("wm_t", P), ("w1", HID), ("w2_t", HID), ("headmask", P), ("pairavg", P), ("ident", P),
    ("fold", C), ("w2e", E * C), ("gw", 2 * E), ("gb", 2 * TB * E), ("rank", 2 * TB * E), ("cols", 32),
]:
    COLS[_name] = (_at, _width)
    _at += _width
NW = _at
B_IM, B_OUT, G1, B1, G2, B2, B1E, B2E = 0, 1, 2, 3, 4, 5, 8, 16
NREP = 6
NSEL = 2 * EP
NORMS = 2 * TB
FAR = 1e30
HEADS = P // HD
RSQRT_GUESS = float(0x5F3759DF - 0x400000 - 0x80000000)

SCHEDULE = [
    ("channel_stats", 0), ("gates", 1), ("gate_exp", 0), ("group_stats", 0), ("group_norm", 0),
    ("choose_1", 1), ("info_mask_0", 1), ("choose_2", 1), ("info_mask_1", 1), ("gate_rows", 1),
    ("info_0", 0), ("low_0", 0), ("first_unit", 0), ("high_0", 1), ("info_1", 1), ("low_1", 1),
    ("high_1", 0), ("conv_out", 0), ("finish_1", 0), ("centre_1", 3), ("rstd_1", 1), ("norm_1_0", 1),
    ("norm_1_1", 1), ("features_1", 0), ("query", 1), ("key", 1), ("value", 0), ("key_value", 0),
    ("denominator", 1), ("numerator", 0), ("attended", 0), ("message", 1), ("rstd_2", 1),
    ("norm_2_0", 0), ("norm_2_1", 2), ("features_2", 0), ("hidden_0", 1), ("hidden_1", 0),
    ("hidden_out", 0), ("tokens_3", 1), ("rstd_3", 2), ("norm_3_0", 0), ("norm_3_1", 1),
    ("features_3", 1), ("finish_0", 0), ("centre_4", 1), ("rstd_4", 1), ("norm_4_0", 1), ("norm_4_1", 1),
    ("features_4_0", 0), ("features_4_1", 0),
]
CHAIN_STEPS = (1 + LNS) * 11
ROUTER_STEPS = 14
ROUTER = ("gates", "gate_exp", "choose_1", "choose_2", "gate_rows", "first_unit")
assert sum(n for _, n in SCHEDULE) == US
TAIL = sum(n for _, n in SCHEDULE[:[name for name, _ in SCHEDULE].index("first_unit")])


def build(nc, x, wpack, w1e, reps, out):
    xd = x.rearrange("(n two) c t -> n (two c) t", two=2)
    od = out.rearrange("(n two) c t -> n (two c) t", two=2)
    with ExitStack() as ctx:
        def sb(name, shape, dt=F32):
            return ctx.enter_context(nc.sbuf_tensor(name, shape, dt))

        def sem(name):
            return ctx.enter_context(nc.semaphore(name))

        def sems(name):
            return [sem(f"{name}{g}") for g in range(G)]

        W = sb("W", [P, NW])
        X = sb("X", [P, G, T])
        XB = sb("XB", [P, 2, G, T])
        XN = sb("XN", [P, G, T])
        T1 = sb("T1", [P, G, T])
        T2 = sb("T2", [P, G, T])
        BIG = sb("BIG", [P, G, 4, T])
        IM = sb("IM", [P, G, T], F32R)
        S = sb("S", [P, 2, G, 2, T], F32R)
        CT = sb("CT", [P, 2, G, T], F32R)
        RT = sb("RT", [P, G, 5 * P + NORMS])
        CHL = sb("CHL", [P, G, 2, P])
        KVM = sb("KVM", [P, G, P])
        KS = sb("KS", [P, G, HEADS])
        RZ = sb("RZ", [P, G, TB, HEADS])
        SM = sb("SM", [P, 4, G, NORMS])
        H = sb("H", [P, 2, 2, CH])
        ACC = sb("ACC", [P, G, 2, T])
        TM = sb("TM", [P, 2, CH])
        CW = sb("CW", [P, 2, CH])
        WMC = sb("WMC", [P, P])
        W2C = sb("W2C", [P, C])
        W1G = sb("W1G", [P, HID])
        BH = sb("BH", [P, 1])
        BT = sb("BT", [P, 1])
        WEH = sb("WEH", [P, E, HID], F32R)
        WEL = sb("WEL", [P, E, HID], F32R)
        REP = sb("REP", [P, NREP + NSEL, P], F32R)
        ST = sb("ST", [P, G, 32])

        def psum(name, columns):
            return ctx.enter_context(nc.psum_tensor(name, [P, columns], F32))

        R = [psum(f"R{s}", T) for s in range(G)]
        HP = [psum(f"HP{e}", CH) for e in range(2)]
        YC = [psum(f"YC{k}", CH) for k in range(2)]

        def w(name, rows=slice(0, P)):
            a, n = COLS[name]
            return W[rows, a:a + n]

        def col(k, rows=slice(0, P)):
            a = COLS["cols"][0] + k
            return W[rows, a:a + 1]

        raw_w1e = BIG[:, 0, 0, :]
        raw_reps = BIG[:, 0, 1:3, :].rearrange("p a t -> p (a t)")[:, 0:(NREP + NSEL) * P]
        XR = XN[:, :, :].bitcast(F32R)

        def half(c):
            return slice(c * CH, (c + 1) * CH)

        def token_blocks(c):
            return slice(c * TB // NCH, (c + 1) * TB // NCH)

        def img(k):
            return slice(k * C, (k + 1) * C)

        Q = [BIG[:, s, 0, :] for s in range(G)]
        K = [BIG[:, s, 1, :] for s in range(G)]
        V = [BIG[:, s, 2:4, :].rearrange("p a t -> p (a t)")[:, 0:TB * VW].rearrange("p (j c) -> p j c", c=VW)
             for s in range(G)]
        U = [[BIG[:, s, k, :] for k in range(2)] for s in range(G)]
        HA = [[BIG[:, s, 2 + k, :] for k in range(2)] for s in range(G)]

        w_in = sem("w_in")
        r_in = sem("r_in")
        ct_zero = sem("ct_zero")
        act_prep = sem("act_prep")
        prep_pe = sem("prep_pe")
        prep_done = sem("prep_done")
        x_in = sems("x_in")
        gn_part = sem("gn_part")
        gn_stat = sem("gn_stat")
        gn_dev = sem("gn_dev")
        gn_avg = sem("gn_avg")
        gn_var = sem("gn_var")
        gn_done = sem("gn_done")
        im_ps = sem("im_ps")
        im_act = sem("im_act")
        hl_high = sem("hl_high")
        hl_done = sem("hl_done")
        rep_ps = sem("rep_ps")
        ir_done = sem("ir_done")
        prod_done = sem("prod_done")
        oc_ps = sem("oc_ps")
        oc_act = sem("oc_act")
        x1_done = sem("x1_done")
        ln_ps = sem("ln_ps")
        ln_sq = sem("ln_sq")
        ln_stat = sem("ln_stat")
        ln_tok = sem("ln_tok")
        ln_back = sem("ln_back")
        xb_part = sem("xb_part")
        xs_done = sem("xs_done")
        msg_norm = sem("msg_norm")
        qk_ps = sem("qk_ps")
        qk_exp = sem("qk_exp")
        qk_min = sem("qk_min")
        qk_done = sem("qk_done")
        v_ps = sem("v_ps")
        v_done = sem("v_done")
        kv_ps = sem("kv_ps")
        kv_done = sem("kv_done")
        den_ps = sem("den_ps")
        den_eps = sem("den_eps")
        den_done = sem("den_done")
        num_ps = sem("num_ps")
        msg_done = sem("msg_done")
        att_ps = sem("att_ps")
        att_done = sem("att_done")
        u_in = sems("u_in")
        h_ps = sem("h_ps")
        h_done = sem("h_done")
        y2_ps = sem("y2_ps")
        y2_done = sem("y2_done")
        x2_done = sem("x2_done")
        xf_done = sem("xf_done")
        sp_high = sem("sp_high")
        sp_low = sem("sp_low")
        s_in = sems("s_in")
        gate_ps = sem("gate_ps")
        lg_done = sem("lg_done")
        lg_shifted = sem("lg_shifted")
        gate_exp = sem("gate_exp")
        cw_done = sem("cw_done")
        cwt_ps = sem("cwt_ps")
        cwt_done = sem("cwt_done")
        ct_in = sems("ct_in")
        l1_ps = sem("l1_ps")
        gelu_done = sem("gelu_done")
        cwb_ps = sem("cwb_ps")
        cwb_done = sem("cwb_done")
        y_ps = sem("y_ps")
        comb_done = sem("comb_done")
        acc_done = sem("acc_done")
        fin_ps = sem("fin_ps")
        fin_done = sem("fin_done")
        out_done = sems("out_done")
        ones_set = sem("ones_set")
        dve_prep = sem("dve_prep")
        chain = sem("chain")
        router = sem("router")
        ct_high = sem("ct_high")


        def pieces(slots):
            return [(s, c) for s in slots for c in range(NCH)]

        PIECES = pieces(range(G))

        def nth(n, s, c=None):
            if c is None:
                return (n - 1) * G + s + 1
            return ((n - 1) * G + s) * NCH + c + 1

        LAST = NCH - 1

        def unit(u):
            return u // CH_UNITS, u // (2 * EP) % 2, u // 2 % EP, u % 2

        ADDS = US // EP * (EP - 1)

        def adds(u):
            return u // (2 * EP) * 2 * (EP - 1) + max(u % (2 * EP) - 2, 0)

        def gt(k):
            return RT[:, :, P * k:P * k + P]

        def rows(t):
            return t.rearrange("p g (r e) -> p g r e", e=E)

        def turn(a, b, c, par, parts):
            stages, started, left = {}, None, None
            if c is not None:
                ends, left = parts(None, c, 1 - par)
                stages["finish_1"] = ends.get("finish_1")
            if b is not None:
                ends, started = parts(None, b, par)
                stages["finish_0"] = ends.get("finish_0")
                routing, _ = parts(b, None, 1 - par)
                stages.update((name, routing.get(name)) for name in ROUTER)
            if a is not None:
                dense, _ = parts(a, None, par)
                stages.update((name, f) for name, f in dense.items()
                              if name not in ROUTER and not name.startswith("finish"))
            u = US - TAIL
            for name, units in SCHEDULE:
                if stages.get(name):
                    stages[name]()
                if name == "first_unit":
                    u, left = 0, started
                for _ in range(units if left else 0):
                    left(u)
                    u += 1
                if not left:
                    u += units

        def turns(eng, parts, apart=0):
            turn(0, None, None, 0, parts)
            turn(1, 0, None, 1, parts)
            with eng.Fori(0, GROUPS // 2 - 1 - apart) as i:
                turn(i * 2 + 2, i * 2 + 1, i * 2, 0, parts)
                turn(i * 2 + 3, i * 2 + 2, i * 2 + 1, 1, parts)
            for a in range(GROUPS - 2 * apart, GROUPS):
                turn(a, a - 1, a - 2, a % 2, parts)
            turn(None, GROUPS - 1, GROUPS - 2, 0, parts)
            turn(None, None, GROUPS - 1, 1, parts)

        def exists(g):
            return not isinstance(g, int) or 0 <= g < GROUPS

        def starting(a):
            return isinstance(a, int) and a == 0

        block = ctx.enter_context(nc.Block())

        @block.sync
        def _(sp):
            for s in range(G):
                sp.dma_start(X[:, s, :], xd[s]).then_inc(x_in[s], 16)
            sp.dma_start(W[:, :], wpack).then_inc(w_in, 16)
            sp.dma_start(raw_reps, reps).then_inc(r_in, 16)
            sp.dma_start(raw_w1e, w1e).then_inc(r_in, 16)

            def parts(a, b, par):
                def attention_input():
                    for s in range(G):
                        sp.wait_ge(num_ps, nth(a + 1, s, LAST))
                        for k in range(2):
                            sp.dma_start(U[s][k][0:C, :], XN[img(k), s, :]).then_inc(u_in[s], 16)

                def next_input():
                    if isinstance(a, int) and a == GROUPS - 1:
                        return
                    for s in range(G):
                        sp.wait_ge(xs_done, nth(a + 1, s))
                        sp.dma_start(X[:, s, :], xd[a * G + G + s]).then_inc(x_in[s], 16)

                def expert_input(s):
                    sp.wait_ge(sp_low, nth(a + 1, s, LAST))
                    for k in range(2):
                        sp.dma_start(S[0:C, par, s, k, :].bitcast(F32), XN[img(k), s, :])\
                            .then_inc(s_in[s], 16)
                        sp.dma_start(S[C:P, par, s, k, :].bitcast(F32), T2[img(k), s, :])\
                            .then_inc(s_in[s], 16)

                def gate_weights():
                    sp.wait_ge(cwt_done, a + 1)
                    for s in range(G):
                        for part in range(2):
                            sp.dma_start(CT[16 * part:16 * part + 16, par, s, :].bitcast(F32),
                                         CHL[:, s, part, :]).then_inc(ct_in[s], 16)

                def store(s):
                    sp.wait_ge(fin_done, (b * G + s + 1) * NCH)
                    sp.dma_start(od[b * G + s], XB[:, 1 - par, s, :]).then_inc(out_done[s], 16)

                return {
                    "features_1": next_input, "message": attention_input,
                    "features_4_0": lambda: expert_input(0), "features_4_1": lambda: expert_input(1),
                    "gate_rows": gate_weights, "finish_0": lambda: store(0),
                    "finish_1": lambda: store(1),
                }, lambda u: None

            turns(sp, parts, apart=1)
            for s in range(G):
                sp.wait_ge(out_done[s], GROUPS * 16)

        @block.tensor
        def _(pe):
            mm = nc.tensor.matmul

            pe.wait_ge(w_in, 16)
            mm(YC[0][:, 0:P], w("wm_t"), w("center"), start=True, stop=True)
            mm(YC[0][:, P:P + C], w("w2_t"), w("center")[:, 0:C], start=True, stop=True)
            mm(YC[0][:, P + C:P + C + 1], w("w1"), col(B1), start=True, stop=True).then_inc(prep_pe, 1)

            def parts(a, b, par):
                def group_stats():
                    for s in range(G):
                        pe.wait_ge(gn_stat, nth(a + 1, s))
                        if exists(a - 1):
                            pe.wait_ge(lg_done, nth(a, s))
                        mm(R[s][:, 0:2], w("pairavg"), ST[:, s, 12:14], start=True, stop=True).then_inc(gn_avg, 1)

                def info_mask(s):
                    pe.wait_ge(gn_done, nth(a + 1, s))
                    for c in range(NCH):
                        mm(R[s][img(c), half(c)], w("wim"), XN[:, s, half(c)], start=True, stop=True)\
                            .then_inc(im_ps, 1)

                def replicate(n):
                    if n == 0 and starting(a):
                        pe.wait_ge(prep_done, 2)
                    for s, c in PIECES:
                        if n == 0:
                            pe.wait_ge(hl_done, nth(a + 1, s, c))
                            if exists(a - 1):
                                pe.wait_ge(cwt_done, a)
                        elif n % 3 == 1:
                            pe.wait_ge(ir_done, nth(a * 2 + n // 3 + 1, s, c))
                        else:
                            pe.wait_ge(prod_done, nth(a * 4 + (n + 1) // 3 + n // 3, s, c))
                        mm(R[s][:, half(c)], REP[:, n, :], IM[:, s, half(c)], start=True, stop=True).then_inc(rep_ps, 1)

                def conv_out():
                    for s, c in PIECES:
                        pe.wait_ge(prod_done, nth(a * 4 + 4, s, c))
                        for h in range(2):
                            for k in range(2):
                                last = mm(R[s][img(k), half(c)], w("ow")[:, C * h:C * h + C],
                                          BIG[:, s, 2 * k + h, half(c)], start=(h == 0), stop=(h == 1))
                        last.then_inc(oc_ps, 1)

                def blocks(c):
                    return range(c * TB // NCH, (c + 1) * TB // NCH)

                def tokens(s, c, src):
                    for j in blocks(c):
                        last = nc.tensor.transpose(R[s][:, P * j:P * j + P], src[:, s, P * j:P * j + P], w("ident"))
                    return last

                def centre_1():
                    for s, c in PIECES:
                        pe.wait_ge(x1_done, nth(a + 1, s, c))
                        if exists(a - 2):
                            pe.wait_ge(fin_done, nth(a - 1, 1, LAST))
                        by_token(s, c, X, w("center")).then_inc(ln_ps, 1)

                def features(k, slots=range(G)):
                    for s, c in pieces(slots):
                        pe.wait_ge(ln_tok, nth(a * LNS + k, s, c))
                        tokens(s, c, T1).then_inc(ln_back, 1)

                def query():
                    for s, c in PIECES:
                        pe.wait_ge(xb_part, nth(a + 1, s, c))
                        mm(R[s][:, half(c)], w("wq"), XN[:, s, half(c)], start=True, stop=True).then_inc(qk_ps, 1)

                def by_token(s, c, src, weights):
                    for j in blocks(c):
                        last = mm(R[s][:, P * j:P * j + P], src[:, s, P * j:P * j + P], weights,
                                  start=True, stop=True)
                    return last

                def key():
                    for s, c in PIECES:
                        pe.wait_ge(qk_done, nth(a * 2 + 1, s, c))
                        by_token(s, c, XN, w("wk")).then_inc(qk_ps, 1)

                def value():
                    for s, c in PIECES:
                        pe.wait_ge(qk_done, nth(a * 2 + 2, s, c))
                        by_token(s, c, XN, w("wv")).then_inc(v_ps, 1)

                def key_value():
                    for s in range(G):
                        pe.wait_ge(v_done, nth(a + 1, s, LAST))
                        pe.wait_ge(ones_set, nth(a + 1, s))
                        for j in range(TB):
                            last = mm(R[s][:, 0:VW], K[s][:, P * j:P * j + P], V[s][:, j, :],
                                      start=(j == 0), stop=(j == TB - 1))
                        last.then_inc(kv_ps, 1)

                def denominator():
                    for s in range(G):
                        pe.wait_ge(kv_done, nth(a + 1, s))
                        for j in range(TB):
                            last = mm(R[s][:, HEADS * j:HEADS * j + HEADS], Q[s][:, P * j:P * j + P], KS[:, s, :],
                                      start=True, stop=True)
                        last.then_inc(den_ps, 1)

                def numerator():
                    for s, c in PIECES:
                        if c == 0:
                            pe.wait_ge(den_eps, nth(a + 1, s))
                        for j in blocks(c):
                            last = mm(R[s][:, P * j:P * j + P], Q[s][:, P * j:P * j + P], KVM[:, s, :],
                                      start=True, stop=True)
                        last.then_inc(num_ps, 1)

                def attended():
                    for s, c in PIECES:
                        pe.wait_ge(msg_done, nth(a + 1, s, c))
                        tokens(s, c, T2).then_inc(att_ps, 1)

                def message():
                    for s, c in PIECES:
                        pe.wait_ge(att_done, nth(a + 1, s, c))
                        by_token(s, c, T1, WMC[:, :]).then_inc(ln_ps, 1)

                def hidden(k):
                    for s, c in PIECES:
                        if k == 0:
                            pe.wait_ge(u_in[s], a * 32 + 32)
                            pe.wait_ge(msg_norm, nth(a + 1, s, c))
                        else:
                            pe.wait_ge(h_done, nth(a * 2 + 1, s, c))
                        mm(R[s][:, half(c)], W1G[:, :], U[s][k][:, half(c)], start=True, stop=True)\
                            .then_inc(h_ps, 1)

                def hidden_out():
                    for s, c in PIECES:
                        pe.wait_ge(h_done, nth(a * 2 + 2, s, c))
                        for k in range(2):
                            last = mm(R[s][img(k), half(c)], W2C[:, :], HA[s][k][:, half(c)],
                                      start=True, stop=True)
                        last.then_inc(y2_ps, 1)

                def tokens_3():
                    for s, c in PIECES:
                        pe.wait_ge(y2_done, nth(a + 1, s, c))
                        tokens(s, c, T1).then_inc(ln_ps, 1)

                def centre_4():
                    for s, c in PIECES:
                        pe.wait_ge(x2_done, nth(a + 1, s, c))
                        if exists(a - 1):
                            pe.wait_ge(fin_done, nth(a, 0, LAST))
                        by_token(s, c, XB[:, par, :, :], w("center")).then_inc(ln_ps, 1)

                def gates():
                    for s, c in PIECES:
                        pe.wait_ge(xf_done, nth(a + 1, s, c))
                        for j in blocks(c):
                            last = mm(R[s][:, 2 * E * j:2 * E * (j + 1)], T1[:, s, P * j:P * j + P], w("gw"),
                                      start=True, stop=True)
                        if c == LAST:
                            last.then_inc(gate_ps, 1)

                def gate_rows():
                    pe.wait_ge(cw_done, a + 1)
                    if exists(a + 1):
                        pe.wait_ge(im_act, nth(a + 2, G - 1, LAST))
                    for s in range(G):
                        last = nc.tensor.transpose(R[s][:, 0:P], RT[:, s, 0:P], w("ident"))
                    last.then_inc(cwt_ps, 1)

                def hidden_layers(g, p, u):
                    s, k, ep, c = unit(u)
                    if u % CH_UNITS == 0:
                        pe.wait_ge(s_in[s], g * 64 + 64)
                    for e in range(2):
                        ex = 2 * ep + e
                        mm(HP[e][:, :], WEH[:, ex, :], S[:, p, s, k, half(c)], start=True, stop=False)
                        mm(HP[e][:, :], WEL[:, ex, :], S[:, p, s, k, half(c)], start=False, stop=True)\
                            .then_inc(l1_ps, 1)

                def gate_weights(u):
                    s, k, ep, c = unit(u)
                    if u % CH_UNITS == 0:
                        pe.wait_ge(ct_in[s], b * 32 + 32)
                    if u >= 2 or not (isinstance(b, int) and b == 0):
                        pe.wait_ge(comb_done, b * US + u - 1)
                    mm(YC[u % 2][:, :], REP[:, NREP + k * EP + ep, :], CT[:, 1 - par, s, half(c)],
                       start=True, stop=True).then_inc(cwb_ps, 1)

                def expert(u):
                    s, k, ep, c = unit(u)
                    if u == 0:
                        gate_weights(0)
                    pe.wait_ge(gelu_done, (b * US + u + 1) * 2)
                    if u + 1 < US:
                        hidden_layers(b, 1 - par, u + 1)
                    pe.wait_ge(cwb_done, b * US + u + 1)
                    for e in range(2):
                        ex = 2 * ep + e
                        last = mm(YC[u % 2][img(e), :], w("w2e")[:, C * ex:C * ex + C], H[:, u % 2, e, :],
                                  start=True, stop=True)
                    last.then_inc(y_ps, 1)
                    if u + 1 < US:
                        gate_weights(u + 1)

                def finish(s):
                    pe.wait_ge(comb_done, b * US + (s + 1) * CH_UNITS)
                    pe.wait_ge(acc_done, b * ADDS + adds((s + 1) * CH_UNITS))
                    if exists(b + 1 + s):
                        pe.wait_ge(oc_act if s else x2_done, nth(b + 2 + s, 0, LAST))
                    for c in range(NCH):
                        for k in range(2):
                            last = mm(R[0][img(k), half(c)], w("fold"), ACC[:, s, k, half(c)], start=True, stop=True)
                        last.then_inc(fin_ps, 1)

                return {
                    "group_stats": group_stats, "info_mask_0": lambda: info_mask(0),
                    "info_mask_1": lambda: info_mask(1), "info_0": lambda: replicate(0),
                    "low_0": lambda: replicate(1), "high_0": lambda: replicate(2),
                    "info_1": lambda: replicate(3), "low_1": lambda: replicate(4),
                    "high_1": lambda: replicate(5), "conv_out": conv_out, "centre_1": centre_1,
                    "features_1": lambda: features(1), "query": query, "key": key, "value": value,
                    "key_value": key_value, "denominator": denominator, "numerator": numerator,
                    "attended": attended, "message": message, "features_2": lambda: features(2),
                    "hidden_0": lambda: hidden(0), "hidden_1": lambda: hidden(1),
                    "hidden_out": hidden_out, "tokens_3": tokens_3, "features_3": lambda: features(3),
                    "centre_4": centre_4, "features_4_0": lambda: features(4, (0,)),
                    "features_4_1": lambda: features(4, (1,)), "gates": gates, "gate_rows": gate_rows,
                    "first_unit": lambda: hidden_layers(a, par, 0), "finish_0": lambda: finish(0),
                    "finish_1": lambda: finish(1),
                }, expert

            turns(pe, parts)

        @block.scalar
        def _(act):
            f = nc.scalar.activation
            act.wait_ge(w_in, 16)
            f(BT[:, :], col(B_IM), ACT.Copy, scale=0.5).then_inc(act_prep, 1)
            act.wait_ge(r_in, 32)
            f(REP[:, :, :], raw_reps.rearrange("p (n c) -> p n c", c=P), ACT.Copy).then_inc(act_prep, 1)
            f(WEH[:, :, :], raw_w1e.rearrange("p (e h) -> p e h", h=HID), ACT.Copy).then_inc(act_prep, 1)
            act.wait_ge(act_prep, 1)

            def parts(a, b, par):
                def info_mask(s):
                    for c in range(NCH):
                        act.wait_ge(im_ps, nth(a + 1, s, c))
                        info, mask = slice(C * c, C * c + 32), slice(C * c + 32, C * c + 64)
                        f(T1[0:32, s, half(c)], R[s][info, half(c)], ACT.Relu, bias=col(B_IM, info))
                        f(T1[32:64, s, half(c)], R[s][mask, half(c)], ACT.Tanh, bias=BT[mask, :], scale=0.5)\
                            .then_inc(im_act, 1)

                def info(k):
                    for s, c in PIECES:
                        act.wait_ge(rep_ps, nth(a * NREP + 3 * k + 1, s, c))
                        f(T2[:, s, half(c)], R[s][:, half(c)], ACT.Copy).then_inc(ir_done, 1)

                def conv_out():
                    for s, c in PIECES:
                        act.wait_ge(oc_ps, nth(a + 1, s, c))
                        f(T1[:, s, half(c)], R[s][:, half(c)], ACT.Relu, bias=col(B_OUT), scale=0.5).then_inc(oc_act, 1)

                def square(k):
                    for s, c in PIECES:
                        act.wait_ge(ln_ps, nth(a * LNS + k, s, c))
                        f(T2[:, s, half(c)], R[s][:, half(c)], ACT.Square).then_inc(ln_sq, 1)

                def features_1():
                    for s, c in PIECES:
                        act.wait_ge(ln_back, nth(a * LNS + 1, s, c))
                        f(XN[:, s, half(c)], R[s][:, half(c)], ACT.Copy)
                        if c == 0 and exists(a - 2):
                            act.wait_ge(out_done[s], a * 16 - 16)
                        f(XB[:, par, s, half(c)], R[s][:, half(c)], ACT.Identity, bias=col(B2)).then_inc(xb_part, 1)

                def message_norm():
                    for s, c in PIECES:
                        act.wait_ge(ln_back, nth(a * LNS + 2, s, c))
                        f(U[s][0][C:P, half(c)], R[s][img(0), half(c)], ACT.Copy)
                        f(U[s][1][C:P, half(c)], R[s][img(1), half(c)], ACT.Copy).then_inc(msg_norm, 1)

                def features_4(s):
                    copy_out(ln_back, a * LNS + 4, T1, xf_done, (s,))
                    for c in range(NCH):
                        act.wait_ge(xf_done, nth(a + 1, s, c))
                        f(XR[:, s, half(c)], T1[:, s, half(c)], ACT.Copy).then_inc(sp_high, 1)

                def copy_out(ready, n, dst, done, slots=range(G)):
                    for s, c in pieces(slots):
                        act.wait_ge(ready, nth(n, s, c))
                        f(dst[:, s, half(c)], R[s][:, half(c)], ACT.Copy).then_inc(done, 1)

                def exponential(n):
                    for s, c in PIECES:
                        act.wait_ge(qk_ps, nth(a * 2 + n, s, c))
                        f(T1[:, s, half(c)], R[s][:, half(c)], ACT.Exp).then_inc(qk_exp, 1)

                def value():
                    for s, c in PIECES:
                        act.wait_ge(v_ps, nth(a + 1, s, c))
                        f(V[s][:, token_blocks(c), 0:P], R[s][:, half(c)].rearrange("p (j c) -> p j c", c=P),
                          ACT.Copy).then_inc(v_done, 1)

                def hidden(k):
                    for s, c in PIECES:
                        act.wait_ge(h_ps, nth(a * 2 + k + 1, s, c))
                        f(HA[s][k][:, half(c)], R[s][:, half(c)], ACT.Relu, bias=BH[:, :]).then_inc(h_done, 1)

                def exponential_of_gates():
                    act.wait_ge(lg_shifted, a + 1)
                    f(gt(1), gt(0), ACT.Exp).then_inc(gate_exp, 1)

                def gelu(g, u):
                    ep = unit(u)[2]
                    for e in range(2):
                        act.wait_ge(l1_ps, (g * US + u) * 2 + e + 1)
                        f(H[:, u % 2, e, :], HP[e][:, :], ACT.Gelu, bias=col(B1E + 2 * ep + e))\
                            .then_inc(gelu_done, 1)

                def gate_weights(u):
                    if u >= 2 or not (isinstance(b, int) and b == 0):
                        act.wait_ge(comb_done, b * US + u - 1)
                    act.wait_ge(cwb_ps, b * US + u + 1)
                    f(CW[:, u % 2, :], YC[u % 2][:, :], ACT.Copy).then_inc(cwb_done, 1)

                def expert(u):
                    if u == 0:
                        gate_weights(0)
                    if u + 1 < US:
                        gelu(b, u + 1)
                        gate_weights(u + 1)

                return {
                    "info_mask_0": lambda: info_mask(0), "info_mask_1": lambda: info_mask(1),
                    "info_0": lambda: info(0), "info_1": lambda: info(1), "conv_out": conv_out,
                    "centre_1": lambda: square(1), "features_1": features_1,
                    "query": lambda: exponential(1), "key": lambda: exponential(2), "value": value,
                    "attended": lambda: copy_out(att_ps, a + 1, T1, att_done),
                    "message": lambda: square(2), "features_2": message_norm,
                    "hidden_0": lambda: hidden(0), "hidden_1": lambda: hidden(1),
                    "hidden_out": lambda: copy_out(y2_ps, a + 1, T1, y2_done),
                    "tokens_3": lambda: square(3), "centre_4": lambda: square(4),
                    "features_4_0": lambda: features_4(0), "features_4_1": lambda: features_4(1),
                    "gate_exp": exponential_of_gates, "first_unit": lambda: gelu(a, 0),
                }, expert

            turns(act, parts)

        @block.gpsimd
        def _(pool):
            nc.gpsimd.memset(CT[:, :, :, :].bitcast(F32), 0.0).then_inc(ct_zero, 1)
            pool.wait_ge(act_prep, 3)
            nc.gpsimd.tensor_tensor(WEL[:, :, :], raw_w1e.rearrange("p (e h) -> p e h", h=HID),
                                    WEH[:, :, :].bitcast(F32), ALU.subtract).then_inc(prep_done, 1)

            def parts(a, b, par):
                def residual():
                    for s in range(G):
                        pool.wait_ge(xb_part, nth(a + 1, s, LAST))
                        nc.gpsimd.tensor_tensor(XB[:, par, s, :], XB[:, par, s, :], X[:, s, :], ALU.add)\
                            .then_inc(xs_done, 1)

                def expert(u):
                    s, k, ep, c = unit(u)
                    if ep:
                        pool.wait_ge(comb_done, b * US + u + 1)
                        acc = ACC[:, s, k, half(c)]
                        nc.gpsimd.tensor_tensor(acc, TM[:, u % 2, :], acc, ALU.add).then_inc(acc_done, 1)

                return {
                    "features_1": residual,
                }, expert

            turns(pool, parts)

        @block.vector
        def _(dve):
            v = nc.vector

            def prepare():
                dve.wait_ge(w_in, 16)
                v.tensor_scalar(W1G[:, :], w("w1"), col(G1), None, ALU.mult).then_inc(dve_prep, 1)
                dve.wait_ge(prep_pe, 1)
                v.tensor_copy(WMC[:, :], YC[0][:, 0:P]).then_inc(dve_prep, 1)
                v.tensor_copy(W2C[:, :], YC[0][:, P:P + C]).then_inc(dve_prep, 1)
                v.tensor_copy(BH[:, :], YC[0][:, P + C:P + C + 1]).then_inc(dve_prep, 1)
                dve.wait_ge(dve_prep, 4)
                dve.wait_ge(ct_zero, 1)
                v.memset(ST[:, 0, 30:31], 0.0).then_inc(prep_done, 1)

            def parts(a, b, par):
                steps = {chain: 0, router: 0}

                def link(ins, signal=chain, per_group=CHAIN_STEPS):
                    steps[signal] += 1
                    ins.then_inc(signal, 1)
                    dve.wait_ge(signal, a * per_group + steps[signal])

                def router_link(ins):
                    link(ins, router, ROUTER_STEPS)

                def rsqrt(n):
                    hz, t, y = (SM[:, k, :, 0:n] for k in (1, 2, 3))
                    link(v.tensor_scalar(y.bitcast(I32), hz.bitcast(I32), -0.5, RSQRT_GUESS, ALU.mult, ALU.add))
                    for _ in range(3):
                        link(v.tensor_tensor(t, y, y, ALU.mult))
                        link(v.tensor_tensor(t, t, hz, ALU.mult))
                        link(v.scalar_tensor_tensor(out=y, in0=t, scalar=-1.5, in1=y, op0=ALU.add, op1=ALU.mult))

                def channel_stats():
                    for s in range(G):
                        dve.wait_ge(x_in[s], a * 16 + 16)
                        for c in range(NCH):
                            ins = v.bn_stats(ST[:, s, 6 * c:6 * c + 6], X[:, s, half(c)])
                        ins.then_inc(gn_part, 1)
                    for s in range(G):
                        dve.wait_ge(gn_part, nth(a + 1, s))
                        v.memset(ST[:, s, 31:32], 0.0)
                        v.bn_aggr(ST[:, s, 12:14], ST[:, s, 0:12]).then_inc(gn_stat, 1)
                    if starting(a):
                        prepare()

                def group_stats():
                    for s in range(G):
                        dve.wait_ge(gn_avg, nth(a + 1, s))
                        dve.wait_ge(gn_stat, nth(a + 1, s))
                        v.tensor_tensor(ST[:, s, 14:15], ST[:, s, 12:13], R[s][:, 0:1], ALU.subtract)\
                            .then_inc(gn_dev, 1)
                    for s in range(G):
                        dve.wait_ge(gn_dev, nth(a + 1, s))
                        v.scalar_tensor_tensor(out=SM[:, 0, s, 0:1], in0=ST[:, s, 14:15], scalar=ST[:, s, 14:15],
                                               in1=R[s][:, 1:2], op0=ALU.mult, op1=ALU.add).then_inc(gn_var, 1)
                    dve.wait_ge(gn_var, nth(a + 1, G - 1))
                    link(v.tensor_scalar(SM[:, 1, :, 0:1], SM[:, 0, :, 0:1], LN_EPS, 0.5, ALU.add, ALU.mult))
                    rsqrt(1)

                def group_norm():
                    for s in range(G):
                        if exists(a - 1):
                            dve.wait_ge(s_in[s], a * 64)
                        v.tensor_scalar(XN[:, s, :], X[:, s, :], R[s][:, 0:1], SM[:, 3, s, 0:1],
                                        ALU.subtract, ALU.mult).then_inc(gn_done, 1)

                def info_mask(s):
                    for c in range(NCH):
                        dve.wait_ge(im_act, nth(a + 1, s, c))
                        high = IM[0:C, s, half(c)]
                        v.tensor_copy(high, T1[0:C, s, half(c)]).then_inc(hl_high, 1)
                        dve.wait_ge(hl_high, nth(a + 1, s, c))
                        v.tensor_tensor(IM[C:P, s, half(c)], T1[0:C, s, half(c)], high.bitcast(F32),
                                        ALU.subtract).then_inc(hl_done, 1)

                def product(k, h):
                    for s, c in PIECES:
                        if h == 0:
                            dve.wait_ge(ir_done, nth(a * 2 + k + 1, s, c))
                        dve.wait_ge(rep_ps, nth(a * NREP + 3 * k + h + 2, s, c))
                        v.scalar_tensor_tensor(out=BIG[:, s, 2 * k + h, half(c)], in0=R[s][:, half(c)], scalar=1.0,
                                               in1=T2[:, s, half(c)], op0=ALU.add, op1=ALU.mult)\
                            .then_inc(prod_done, 1)

                def conv_out():
                    for s, c in PIECES:
                        dve.wait_ge(oc_act, nth(a + 1, s, c))
                        v.tensor_tensor(X[:, s, half(c)], X[:, s, half(c)], T1[:, s, half(c)], ALU.add)\
                            .then_inc(x1_done, 1)
                        if c == LAST:
                            v.memset(V[s][:, :, P:VW], 1.0).then_inc(ones_set, 1)

                def norms(t):
                    return t.rearrange("p (n c) -> p n c", c=C)

                def some_norms(c):
                    return slice(c * NORMS // NCH, (c + 1) * NORMS // NCH)

                def squares(k):
                    for s, c in PIECES:
                        dve.wait_ge(ln_sq, nth(a * LNS + k, s, c))
                        v.reduce_sum(SM[:, 0, s, some_norms(c)], norms(T2[:, s, half(c)]), AX_X).then_inc(ln_stat, 1)

                def rstd(k):
                    dve.wait_ge(ln_stat, nth(a * LNS + k, G - 1, LAST))
                    link(v.tensor_scalar(SM[:, 1, :, :], SM[:, 0, :, :], 0.5 / C, 0.5 * LN_EPS,
                                         ALU.mult, ALU.add))
                    rsqrt(NORMS)

                def scale(s):
                    for c in range(NCH):
                        v.tensor_tensor(norms(T1[:, s, half(c)]), norms(R[s][:, half(c)]),
                                        SM[:, 3, s, some_norms(c)].unsqueeze(2)
                                        .broadcast_to([P, NORMS // NCH, C]), ALU.mult).then_inc(ln_tok, 1)

                def elu_plus_one(n, dst):
                    for s, c in PIECES:
                        dve.wait_ge(qk_exp, nth(a * 2 + n, s, c))
                        v.tensor_scalar(T1[:, s, half(c)], T1[:, s, half(c)], 1.0, None, ALU.min).then_inc(qk_min, 1)
                    for s, c in PIECES:
                        dve.wait_ge(qk_min, nth(a * 2 + n, s, c))
                        v.scalar_tensor_tensor(out=dst[s][:, half(c)], in0=R[s][:, half(c)], scalar=0.0, in1=T1[:, s, half(c)],
                                               op0=ALU.max, op1=ALU.add).then_inc(qk_done, 1)

                def key_value():
                    for s in range(G):
                        dve.wait_ge(kv_ps, nth(a + 1, s))
                        v.tensor_tensor(KVM[:, s, :], R[s][:, 0:P], w("headmask"), ALU.mult)
                        v.tensor_scalar(KS[:, s, :], w("headmask").rearrange("p (h d) -> p h d", d=HD)[:, :, 0],
                                        R[s][:, P:P + 1], None, ALU.mult)\
                            .then_inc(kv_done, 1)

                def denominator():
                    for s in range(G):
                        dve.wait_ge(den_ps, nth(a + 1, s))
                        v.tensor_scalar(RZ[:, s, :, :], R[s][:, 0:TB * HEADS].rearrange("p (j h) -> p j h", h=HEADS),
                                        ATT_EPS, None, ALU.add).then_inc(den_eps, 1)
                    for s in range(G):
                        dve.wait_ge(den_eps, nth(a + 1, s))
                        v.reciprocal(RZ[:, s, :, :], RZ[:, s, :, :]).then_inc(den_done, 1)

                def numerator():
                    for s, c in PIECES:
                        if c == 0:
                            dve.wait_ge(den_done, nth(a + 1, s))
                        dve.wait_ge(num_ps, nth(a + 1, s, c))
                        v.tensor_tensor(T2[:, s, half(c)].rearrange("p (h d) -> p h d", d=HD),
                                        R[s][:, half(c)].rearrange("p (h d) -> p h d", d=HD),
                                        RZ[:, s, token_blocks(c), :].rearrange("p j h -> p (j h)").unsqueeze(2)
                                        .broadcast_to([P, TB * HEADS // NCH, HD]), ALU.mult).then_inc(msg_done, 1)

                def features_3():
                    for s, c in PIECES:
                        if c == 0:
                            dve.wait_ge(xs_done, nth(a + 1, s))
                        dve.wait_ge(ln_back, nth(a * LNS + 3, s, c))
                        v.scalar_tensor_tensor(out=XB[:, par, s, half(c)], in0=R[s][:, half(c)], scalar=col(G2),
                                               in1=XB[:, par, s, half(c)], op0=ALU.mult, op1=ALU.add)\
                            .then_inc(x2_done, 1)

                def features_4(s):
                    for c in range(NCH):
                        dve.wait_ge(sp_high, nth(a + 1, s, c))
                        v.tensor_tensor(T2[:, s, half(c)], T1[:, s, half(c)], XN[:, s, half(c)], ALU.subtract)\
                            .then_inc(sp_low, 1)

                best = RT[:, :, 5 * P:5 * P + NORMS]
                def per_token(t):
                    return t.unsqueeze(3).broadcast_to([P, G, 2 * TB, E])

                def first_largest(values, chosen):
                    router_link(v.scalar_tensor_tensor(out=chosen, in0=values, scalar=0.0, op0=ALU.is_equal, op1=ALU.mult,
                                                in1=w("rank").unsqueeze(1).broadcast_to([P, G, P])))
                    router_link(v.reduce_max(best, rows(chosen), AX_X))
                    router_link(v.tensor_tensor(rows(chosen), rows(chosen), per_token(best), ALU.is_equal))

                def below_largest(t):
                    router_link(v.reduce_max(best, rows(t), AX_X))
                    return v.tensor_tensor(rows(t), rows(t), per_token(best), ALU.subtract)

                def gates():
                    for s in range(G):
                        dve.wait_ge(gate_ps, nth(a + 1, s))
                        v.tensor_tensor(RT[:, s, 0:P], R[s][:, 0:P], w("gb"), ALU.add).then_inc(lg_done, 1)
                    dve.wait_ge(lg_done, nth(a + 1, G - 1))
                    below_largest(gt(0)).then_inc(lg_shifted, 1)

                def choose_1():
                    dve.wait_ge(lg_shifted, a + 1)
                    first_largest(gt(0), gt(2))
                    router_link(v.scalar_tensor_tensor(out=gt(3), in0=gt(2), scalar=-FAR, in1=gt(0),
                                                op0=ALU.mult, op1=ALU.add))

                def choose_2():
                    router_link(below_largest(gt(3)))
                    first_largest(gt(3), gt(4))
                    router_link(v.tensor_tensor(gt(2), gt(2), gt(4), ALU.add))
                    dve.wait_ge(gate_exp, a + 1)
                    router_link(v.tensor_tensor(gt(2), gt(2), gt(1), ALU.mult))
                    router_link(v.reduce_sum(best, rows(gt(1)), AX_X))
                    router_link(v.reciprocal(best, best))
                    for s in range(G):
                        for k in range(2):
                            ins = v.tensor_tensor(
                                RT[:, s, k * C:k * C + C].rearrange("p (e j) -> p j e", e=E),
                                RT[:, s, 2 * P:3 * P].rearrange("p (j k e) -> p j k e", k=2, e=E)[:, :, k, :],
                                best[:, s, :].rearrange("p (j k) -> p j k", k=2)[:, :, k].unsqueeze(2)
                                .broadcast_to([P, TB, E]), ALU.mult)
                    ins.then_inc(cw_done, 1)

                def gate_rows():
                    assert steps[router] == ROUTER_STEPS
                    dve.wait_ge(cwt_ps, a + 1)
                    for s in range(G):
                        ins = v.tensor_copy(CHL[:, s, 0, :].bitcast(F32R), R[s][:, 0:P])
                    ins.then_inc(ct_high, 1)
                    dve.wait_ge(ct_high, a + 1)
                    for s in range(G):
                        ins = v.tensor_tensor(CHL[:, s, 1, :], R[s][:, 0:P], CHL[:, s, 0, :], ALU.subtract)
                    ins.then_inc(cwt_done, 1)

                def expert(u):
                    s, k, ep, c = unit(u)
                    if ep and (adds(u - 1) or exists(b - 1)):
                        dve.wait_ge(acc_done, b * ADDS + adds(u - 1))
                    dve.wait_ge(y_ps, b * US + u + 1)
                    dve.wait_ge(cwb_done, b * US + u + 1)
                    dst = TM[:, u % 2, :] if ep else ACC[:, s, k, half(c)]
                    v.scalar_tensor_tensor(out=dst, in0=YC[u % 2][:, :], scalar=col(B2E + ep), in1=CW[:, u % 2, :],
                                           op0=ALU.add, op1=ALU.mult).then_inc(comb_done, 1)

                def finish(s):
                    for c in range(NCH):
                        dve.wait_ge(fin_ps, nth(b + 1, s, c))
                        x = XB[:, 1 - par, s, half(c)]
                        v.tensor_tensor(x, R[0][:, half(c)], x, ALU.add).then_inc(fin_done, 1)

                return {
                    "channel_stats": channel_stats, "group_stats": group_stats, "group_norm": group_norm,
                    "info_mask_0": lambda: info_mask(0), "info_mask_1": lambda: info_mask(1),
                    "low_0": lambda: product(0, 0), "high_0": lambda: product(0, 1),
                    "low_1": lambda: product(1, 0), "high_1": lambda: product(1, 1),
                    "conv_out": conv_out, "centre_1": lambda: squares(1), "rstd_1": lambda: rstd(1),
                    "norm_1_0": lambda: scale(0), "norm_1_1": lambda: scale(1),
                    "query": lambda: elu_plus_one(1, Q), "key": lambda: elu_plus_one(2, K),
                    "key_value": key_value, "denominator": denominator, "numerator": numerator,
                    "message": lambda: squares(2), "rstd_2": lambda: rstd(2),
                    "norm_2_0": lambda: scale(0), "norm_2_1": lambda: scale(1),
                    "tokens_3": lambda: squares(3), "rstd_3": lambda: rstd(3),
                    "norm_3_0": lambda: scale(0), "norm_3_1": lambda: scale(1), "features_3": features_3,
                    "centre_4": lambda: squares(4), "rstd_4": lambda: rstd(4),
                    "norm_4_0": lambda: scale(0), "norm_4_1": lambda: scale(1),
                    "features_4_0": lambda: features_4(0), "features_4_1": lambda: features_4(1),
                    "gates": gates, "choose_1": choose_1, "choose_2": choose_2, "gate_rows": gate_rows,
                    "finish_0": lambda: finish(0), "finish_1": lambda: finish(1),
                }, expert

            turns(dve, parts)


def kernel(**inputs):
    import concourse.bacc as bacc
    from concourse.bass_utils import run_bass_kernel_spmd

    f = lambda n: np.asarray(inputs[n])
    wp = np.zeros((P, NW), np.float32)

    def put(name, a, rows=0, at=0):
        a = np.atleast_2d(a)
        c = COLS[name][0] + at
        wp[rows:rows + a.shape[0], c:c + a.shape[1]] = a

    info, mask, ow = f("L0_conv_info_w"), f("L0_conv_mask_w"), f("L0_conv_out_w")
    wm, w1, w2 = f("L1_attn_Wm"), f("L1_attn_W1"), f("L1_attn_W2")
    centre = np.eye(C, dtype=np.float32) - np.float32(1 / C)
    for k in range(2):
        r = k * C
        put("wim", info.T, r, IC * k)
        put("wim", mask.T, r, 2 * IC + IC * k)
        put("center", centre, r, r)
        put("wq", f("L1_attn_Wq"), r, r)
        put("wk", f("L1_attn_Wk"), r, r)
        put("wv", f("L1_attn_Wv"), r, r)
        put("wm_t", wm.T, r, r)
        put("gw", f("L1_ffn_gate_w"), r, E * k)
        put("fold", np.eye(C, dtype=np.float32), r)
        for c in range(NCH):
            put("cols", f("L0_conv_info_b")[:, None], C * c + IC * k, B_IM)
            put("cols", f("L0_conv_mask_b")[:, None], C * c + 2 * IC + IC * k, B_IM)
        put("cols", f("L0_conv_out_b")[:, None], r, B_OUT)
        put("cols", f("L1_attn_g2")[:, None], r, G2)
        put("cols", f("L1_attn_b2")[:, None], r, B2)
    for h in range(2):
        put("ow", ow.T[P * h:P * h + P], 0, C * h)
    put("w1", w1)
    put("w2_t", w2.T)
    put("headmask", np.kron(np.eye(P // HD), np.ones((HD, HD))).astype(np.float32))
    put("pairavg", np.kron(np.eye(C), np.full((2, 2), 0.5)).astype(np.float32))
    put("ident", np.eye(P, dtype=np.float32))
    put("cols", np.ones((C, 1), np.float32), 0, G1)
    put("cols", f("L1_attn_g1")[:, None], C, G1)
    put("cols", f("L1_attn_b1")[:, None], C, B1)
    put("gb", np.broadcast_to(np.tile(f("L1_ffn_gate_b"), 2 * TB), (P, 2 * TB * E)))
    put("rank", np.broadcast_to(np.tile(np.arange(E, 0, -1, dtype=np.float32), 2 * TB), (P, 2 * TB * E)))
    we1, we2 = f("L1_ffn_W1"), f("L1_ffn_W2")
    for e in range(E):
        put("w2e", we2[e], 0, C * e)
        put("cols", f("L1_ffn_b1")[e][:, None], 0, B1E + e)
        put("cols", f("L1_ffn_b2")[e][:, None], C * (e % 2), B2E + e // 2)
    w1e = np.concatenate([we1.transpose(1, 0, 2).reshape(C, E * HID)] * 2, axis=0)
    reps = np.zeros((P, NREP + NSEL, P), np.float32)
    for k in range(2):
        for part in range(2):
            for o in range(P):
                reps[C * part + IC * k + o % IC, 3 * k, o] = 1
                for h in range(2):
                    reps[C * part + 2 * IC + IC * k + o // IC + HD * h, 3 * k + 1 + h, o] = 1
                for ep in range(EP):
                    reps[16 * part + E * k + 2 * ep + o // C, NREP + EP * k + ep, o] = 1

    nc = bacc.Bacc("TRN2", target_bir_lowering=False, num_devices=1)
    xs = f("x")
    arrays = {"x": np.ascontiguousarray(xs.reshape(IMGS, C, T)), "wpack": wp,
              "w1e": np.ascontiguousarray(w1e), "reps": reps.reshape(P, -1)}
    aps = [nc.dram_tensor(n, a.shape, F32, kind="ExternalInput").ap() for n, a in arrays.items()]
    out = nc.dram_tensor("out", (IMGS, C, T), F32, kind="ExternalOutput").ap()
    build(nc, *aps, out)
    r = run_bass_kernel_spmd(nc, [arrays], core_ids=[0])
    return r.results[0]["out"].reshape(xs.shape)
```
